# Optimizing a Trainium2 kernel written in Bass

```python
import numpy as np
import jax
import jax.numpy as jnp

def _softmax(x, axis=-1):
    return jax.nn.softmax(x, axis=axis)

def _gelu(x):
    return jax.nn.gelu(x, approximate=True)

def _silu(x):
    return jax.nn.silu(x)

def _sigmoid(x):
    return jax.nn.sigmoid(x)

def _layernorm(x, axis=-1, eps=1e-05):
    m = jnp.mean(x, axis=axis, keepdims=True)
    v = jnp.var(x, axis=axis, keepdims=True)
    return (x - m) / jnp.sqrt(v + eps)

def _scatter_add(tgt, idx, src, axis=0):
    return tgt.at[idx].add(src)

def _segment_sum(src, seg, n):
    return jax.ops.segment_sum(src, seg, n)
kernel_name = 'mk_recurrent_d1_jaxref_r8_ba447c'

def setup_inputs(seed: int=0):
    np.random.seed(seed)
    _w = jnp.asarray

    def _L0_attn_setup():
        import jax, jax.numpy as jnp
        import numpy as np
        EMBED_DIM = 128
        NUM_HEADS = 16
        NUM_GLOBAL = 4
        NUM_LOCAL = NUM_HEADS - NUM_GLOBAL
        WINDOW = 32
        HEAD_DIM = EMBED_DIM // NUM_HEADS

        def _masks(seq_len):
            i = jnp.arange(seq_len)[:, None]
            j = jnp.arange(seq_len)[None, :]
            diff = i - j
            global_mask = diff < 0
            local_mask = (diff < 0) | (diff > WINDOW)
            return (global_mask, local_mask)

        def _attend(q, k, v, mask):
            scores = jnp.einsum('bhqd,bhkd->bhqk', q, k) * HEAD_DIM ** (-0.5)
            scores = jnp.where(mask[None, None], -jnp.inf, scores)
            w = jax.nn.softmax(scores, axis=-1)
            return jnp.einsum('bhqk,bhkd->bhqd', w, v)
        key = jax.random.key(seed)
        k1, k2, k3 = jax.random.split(key, 3)
        B, S = (4, 256)
        x = jax.random.normal(k1, (B, S, EMBED_DIM), dtype=jnp.float32)
        w_qkv = jax.random.normal(k2, (EMBED_DIM, 3 * EMBED_DIM), dtype=jnp.float32) * EMBED_DIM ** (-0.5)
        b_qkv = jnp.zeros((3 * EMBED_DIM,), dtype=jnp.float32)
        w_out = jax.random.normal(k3, (EMBED_DIM, EMBED_DIM), dtype=jnp.float32) * EMBED_DIM ** (-0.5)
        b_out = jnp.zeros((EMBED_DIM,), dtype=jnp.float32)
        return {'x': x, 'w_qkv': w_qkv, 'b_qkv': b_qkv, 'w_out': w_out, 'b_out': b_out}
    _L0_attn_in = _L0_attn_setup()

    def _L0_ffn_setup():
        import jax, jax.numpy as jnp
        import numpy as np
        E = 16
        K = 4
        NG = 4
        TG = 2
        SCALE = 2.5
        NORM_TOPK = True
        H = 128
        I = 64
        SH_I = I * 2
        B, S = (2, 256)
        key = jax.random.key(seed)
        ks = jax.random.split(key, 9)

        def w(k, shape, fan_in):
            return jax.random.normal(k, shape, jnp.float32) * (1.0 / np.sqrt(fan_in))
        return {'hidden_states': jax.random.normal(ks[0], (B, S, H), jnp.float32), 'gate_w': w(ks[1], (E, H), H), 'gate_bias': jnp.zeros((E,), jnp.float32), 'Wg': w(ks[2], (E, I, H), H), 'Wu': w(ks[3], (E, I, H), H), 'Wd': w(ks[4], (E, H, I), I), 'Ws_g': w(ks[5], (SH_I, H), H), 'Ws_u': w(ks[6], (SH_I, H), H), 'Ws_d': w(ks[7], (H, SH_I), SH_I)}
    _L0_ffn_in = _L0_ffn_setup()
    _d = {'L0_attn_x': _L0_attn_in['x'], 'L0_attn_w_qkv': _L0_attn_in['w_qkv'], 'L0_attn_b_qkv': _L0_attn_in['b_qkv'], 'L0_attn_w_out': _L0_attn_in['w_out'], 'L0_attn_b_out': _L0_attn_in['b_out'], 'L0_ffn_gate_w': _L0_ffn_in['gate_w'], 'L0_ffn_gate_bias': _L0_ffn_in['gate_bias'], 'L0_ffn_Wg': _L0_ffn_in['Wg'], 'L0_ffn_Wu': _L0_ffn_in['Wu'], 'L0_ffn_Wd': _L0_ffn_in['Wd'], 'L0_ffn_Ws_g': _L0_ffn_in['Ws_g'], 'L0_ffn_Ws_u': _L0_ffn_in['Ws_u'], 'L0_ffn_Ws_d': _L0_ffn_in['Ws_d']}
    _x0 = _d['L0_attn_x']
    _d['L0_attn_x'] = jax.random.normal(jax.random.fold_in(jax.random.key(seed), 1), (4, 1024, 128), dtype=_x0.dtype)
    del _x0
    return _d

def reference(L0_attn_x, L0_attn_w_qkv, L0_attn_b_qkv, L0_attn_w_out, L0_attn_b_out, L0_ffn_gate_w, L0_ffn_gate_bias, L0_ffn_Wg, L0_ffn_Wu, L0_ffn_Wd, L0_ffn_Ws_g, L0_ffn_Ws_u, L0_ffn_Ws_d):

    def _L0_attn_ref(x, w_qkv, b_qkv, w_out, b_out):
        import jax, jax.numpy as jnp
        import numpy as np
        EMBED_DIM = 128
        NUM_HEADS = 16
        NUM_GLOBAL = 4
        NUM_LOCAL = NUM_HEADS - NUM_GLOBAL
        WINDOW = 32
        HEAD_DIM = EMBED_DIM // NUM_HEADS

        def _masks(seq_len):
            i = jnp.arange(seq_len)[:, None]
            j = jnp.arange(seq_len)[None, :]
            diff = i - j
            global_mask = diff < 0
            local_mask = (diff < 0) | (diff > WINDOW)
            return (global_mask, local_mask)

        def _attend(q, k, v, mask):
            scores = jnp.einsum('bhqd,bhkd->bhqk', q, k) * HEAD_DIM ** (-0.5)
            scores = jnp.where(mask[None, None], -jnp.inf, scores)
            w = jax.nn.softmax(scores, axis=-1)
            return jnp.einsum('bhqk,bhkd->bhqd', w, v)
        B, S, _ = x.shape
        qkv = x @ w_qkv + b_qkv
        q, k, v = jnp.split(qkv, 3, axis=-1)

        def heads(t):
            return t.reshape(B, S, NUM_HEADS, HEAD_DIM).transpose(0, 2, 1, 3)
        q, k, v = (heads(q), heads(k), heads(v))
        gmask, lmask = _masks(S)
        ctx_g = _attend(q[:, :NUM_GLOBAL], k[:, :NUM_GLOBAL], v[:, :NUM_GLOBAL], gmask)
        ctx_l = _attend(q[:, NUM_GLOBAL:], k[:, NUM_GLOBAL:], v[:, NUM_GLOBAL:], lmask)
        ctx = jnp.concatenate([ctx_g, ctx_l], axis=1)
        ctx = ctx.transpose(0, 2, 1, 3).reshape(B, S, EMBED_DIM)
        return ctx @ w_out + b_out

    def _L0_ffn_ref(hidden_states, gate_w, gate_bias, Wg, Wu, Wd, Ws_g, Ws_u, Ws_d):
        import jax, jax.numpy as jnp
        import numpy as np
        E = 16
        K = 4
        NG = 4
        TG = 2
        SCALE = 2.5
        NORM_TOPK = True
        H = 128
        I = 64
        SH_I = I * 2
        B, S = (2, 256)
        x = hidden_states
        b, s, h = x.shape
        n = b * s
        xf = x.reshape(n, h)
        logits = xf @ gate_w.T
        scores = jax.nn.sigmoid(logits)
        sfc = scores + gate_bias
        epg = E // NG
        grp = sfc.reshape(n, NG, epg)
        g_scores = jax.lax.top_k(grp, 2)[0].sum(-1)
        _, gidx = jax.lax.top_k(g_scores, TG)
        gmask = jax.nn.one_hot(gidx, NG, dtype=sfc.dtype).sum(1)
        emask = jnp.repeat(gmask, epg, axis=1)
        masked = jnp.where(emask > 0, sfc, -jnp.inf)
        _, topk_idx = jax.lax.top_k(masked, K)
        topk_w = jnp.take_along_axis(scores, topk_idx, axis=1)
        if K > 1 and NORM_TOPK:
            topk_w = topk_w / (topk_w.sum(-1, keepdims=True) + 1e-20)
        topk_w = topk_w * SCALE
        cw = (jax.nn.one_hot(topk_idx, E, dtype=topk_w.dtype) * topk_w[..., None]).sum(1)
        hg = jnp.einsum('nh,eih->nei', xf, Wg)
        hu = jnp.einsum('nh,eih->nei', xf, Wu)
        act = jax.nn.silu(hg) * hu
        y = jnp.einsum('nei,ne,ehi->nh', act, cw, Wd)
        shared = jax.nn.silu(xf @ Ws_g.T) * (xf @ Ws_u.T) @ Ws_d.T
        y = y + shared
        return (x + y.reshape(b, s, h)).astype(hidden_states.dtype)
    x = L0_attn_x
    xn = _layernorm(x, axis=-1)
    s = _L0_attn_ref(xn, L0_attn_w_qkv, L0_attn_b_qkv, L0_attn_w_out, L0_attn_b_out)
    g = _silu(_L0_ffn_ref(xn, L0_ffn_gate_w, L0_ffn_gate_bias, L0_ffn_Wg, L0_ffn_Wu, L0_ffn_Wd, L0_ffn_Ws_g, L0_ffn_Ws_u, L0_ffn_Ws_d))
    x = x + s * g
    return x

_drawn_inputs = setup_inputs


def setup_inputs(seed=0):
    import zlib

    import numpy as np

    out = dict(_drawn_inputs(seed))
    spreads = {'L0_attn_b_qkv': (0.0, 0.1), 'L0_attn_b_out': (0.0, 0.1), 'L0_ffn_gate_bias': (0.0, 0.1)}
    factors = {}
    for name, (base, spread) in spreads.items():
        noise = np.random.default_rng([zlib.crc32(name.encode()), seed]).standard_normal(out[name].shape)
        drawn = base * np.exp(spread * noise) if base else spread * noise
        out[name] = jnp.asarray(drawn.astype(out[name].dtype))
    for name, factor in factors.items():
        out[name] = (out[name] * factor).astype(out[name].dtype)
    return out
```

```python
from contextlib import ExitStack

import concourse.bass as bass
from concourse import mybir

F32 = mybir.dt.float32
F32R = mybir.dt.float32r
F16 = mybir.dt.float16
BF16 = mybir.dt.bfloat16
ALU = mybir.AluOpType
ACT = mybir.ActivationFunctionType
AX_X = mybir.AxisListType.X

P = 128
B, S, D = 4, 1024, 128
H, HD = 16, 8
HG = H // 4
WINDOW = 32
BLK = 32
NBLK = S // BLK
CH = 512
NCH = S // CH
TPC = CH // P
NT = S // P
BPC = CH // BLK
LOC = CH // (2 * BLK)
E, TOPK, NGRP, TOPG = 16, 4, 4, 2
I = 64
EP = E // 2
NUP = EP + 1
ROUTE_SCALE = 2.5
LN_EPS = 1e-5
Q_SCALE = float(HD) ** -0.5
QTR = 256

WORK = 6
LAG_PV = 4
LAG_DOWN = 2
NPROB = 6
NHID = 3

C32 = {"ident": 128, "vmask": HG * BLK, "eye32": BLK, "onerow": 1, "lower": NGRP * NGRP}
CR = {"pairsel": EP * P, "repeat": 4 * P}
C16 = {"q_a": HG * P, "q_b": HG * P, "k_a": HG * P, "k_b": HG * P, "negmax": P}
CBF = {"identb": 128, "win": CH, "win0": CH}


def fields(sizes):
    at, out = 0, {}
    for name, n in sizes.items():
        out[name] = (at, at + n)
        at += n
    return out, at


def global_tiles():
    return [(j, c, max(BLK * j, CH * c), CH * (c + 1) - max(BLK * j, CH * c))
            for j in range(NBLK) for c in range(j // BPC, NCH)]


def global_max_tiles():
    return [(j, c, min(CH, BLK * (j + 1) - CH * c)) for j in range(NBLK) for c in range(j // BPC + 1)]


GT, GM = global_tiles(), global_max_tiles()
SCORES = [len(GT)] + [NBLK // LOC] * (HG - 1)
SCORES_BEFORE = [sum(SCORES[:g]) for g in range(HG + 1)]
MAXES = [len(GM)] + [NBLK // LOC] * (HG - 1)


def merged(a, b):
    out, i = [], 0
    for n, step in enumerate(a):
        out.append(step)
        while i < len(b) and (i + 1) * len(a) <= (n + 1) * len(b):
            out.append(b[i])
            i += 1
    return out + b[i:]


def weight_steps():
    return [("weights", kind, lo, min(lo + 4, NUP)) for kind in range(3) for lo in range(0, NUP, 4)] + [("small",)]


def prepare_steps(c):
    return [("xT", c), ("q", c), ("k", c)] + [("vn", c)] + [("v", c, i) for i in range(4)]


def heads_ready(g):
    return ([("qsel", g, c) for c in range(NCH)] + [("ksel", g, c) for c in range(NCH)] + [("pads", g)]
            + [("max", g, n) for n in range(MAXES[g])] + [("maxdone", g)])


def attention_steps():
    out = [("gate",)] + heads_ready(0) + [("qfull", 0, c) for c in range(NCH)]
    for g in range(HG):
        run = []
        for n in range(SCORES[g] + LAG_PV):
            if n < SCORES[g]:
                run.append(("score", g, n))
            if n >= LAG_PV:
                run.append(("pv", g, n - LAG_PV))
        extra = heads_ready(g + 1) if g + 1 < HG else []
        if g == 0:
            extra = extra + [("cwT", c) for c in range(NCH)]
        out += merged(run, extra)
        out.append(("norm", g))
        if g + 1 < HG:
            out += [("qfull", g + 1, c) for c in range(NCH)]
    return out + [("proj", c) for c in range(NCH)]


def expert_steps(c):
    out = []
    for t in range(NUP + LAG_DOWN):
        if t < NUP:
            out.append(("up", c, t))
        if t >= LAG_DOWN:
            out.append(("down", c, t - LAG_DOWN))
    return out + [("z", c)]


def batch_steps(more):
    first, second = expert_steps(0), expert_steps(1)
    if more:
        first = merged(first, [("stats",), ("ln", 0), ("ln", 1)])
        second = merged(second, prepare_steps(0))
    return (attention_steps() + first + second[:8] + [("outT", 0)] + second[8:]
            + (prepare_steps(1) if more else []) + [("outT", 1)])


class Section:

    def __init__(self, steps):
        self.steps, self.place = steps, {}
        self.fills, self.empties = [0] * (WORK + 2), [0] * (WORK + 2)
        turn = 0
        for s in steps:
            if s[0] in ("pv", "down") and s[2] == 0:
                self.add(("acc", s[1]) if s[0] == "pv" else ("y", s[1]), WORK + s[1] % 2, 0)
            if s[0] in ("pv", "down", "norm", "z", "ln", "stats", "pads", "maxdone"):
                continue
            parts = [s] if s[0] != "up" else [s + (x,) for x in ("gate", "up", "weight")[:2 + (s[2] < EP)]]
            for part in parts:
                self.add(part, turn % WORK, 1)
                turn += 1

    def add(self, tile, bank, signalled):
        self.place[tile] = (bank, self.fills[bank], self.empties[bank])
        self.fills[bank] += signalled
        self.empties[bank] += 1


FIRST = Section(weight_steps() + [("stats",), ("ln", 0), ("ln", 1)] + prepare_steps(0) + prepare_steps(1))
BODY = Section(batch_steps(True))
LAST = Section(batch_steps(False))


class At:

    def __init__(self, section, b):
        self.section, self.b, self.steps = section, b, section.steps
        self.next = 0 if section is FIRST else b + 1

    def bank(self, tile):
        return self.section.place[tile][0]

    def filled(self, tile):
        bank, fills, _ = self.section.place[tile]
        if self.section is FIRST:
            return fills + 1
        return self.b * BODY.fills[bank] + (FIRST.fills[bank] + fills + 1)

    def free(self, tile):
        bank, _, empties = self.section.place[tile]
        if self.section is FIRST:
            return empties + 1
        return self.b * BODY.empties[bank] + (FIRST.empties[bank] + empties + 1)

    def taken(self, tile):
        return self.free(tile) + 1


def build(nc, x, w_qkv, b_qkv, w_out, b_out, gate_w, gate_bias, Wg, Wu, Wd, Ws_g, Ws_u, Ws_d,
          c32, cr, c16, out):
    with ExitStack() as ctx:
        def sb(name, shape, dt=F32):
            return ctx.enter_context(nc.sbuf_tensor(name, shape, dt))

        def sem(name):
            return ctx.enter_context(nc.semaphore(name))

        banks = [ctx.enter_context(nc.psum_tensor(f"bank{i}", [P, CH], F32)) for i in range(WORK + 2)]

        f32at, n32 = fields(C32)
        f16at, n16 = fields(C16)
        bfat, nbf = fields(CBF)
        frat, nfr = fields(CR)
        k32, k16, kbf = sb("k32", [P, n32]), sb("k16", [P, n16], F16), sb("kbf", [P, nbf], BF16)

        def const32(name):
            return k32[:, f32at[name][0]:f32at[name][1]]

        def const16(name, g=0):
            return k16[:, f16at[name][0] + g * P:f16at[name][0] + (g + 1) * P]

        def constbf(name):
            return kbf[:, bfat[name][0]:bfat[name][1]]

        ident = const32("ident")
        vmask = const32("vmask").rearrange("p (g c) -> p g c", g=HG)
        stage = sb("stage", [P, 3, NUP, P])
        up_hi = sb("up_hi", [P, 2, NUP, P], F32R)
        up_lo = sb("up_lo", [P, 2, NUP, P], F32R)
        down_w = sb("down_w", [P, NUP, P])
        wqkv = sb("wqkv", [P, 3 * D])
        wqk_hi = sb("wqk_hi", [P, 2 * D], F32R)
        wqk_lo = sb("wqk_lo", [P, 2 * D], F32R)
        wout = sb("wout", [P, D])
        gate_nat = sb("gate_nat", [E, D])
        gateT = sb("gateT", [P, E])
        bias3 = sb("bias3", [P, 3])
        bq = sb("bq", [P, 1])
        bo = sb("bo", [P, 1])
        bs = sb("bs", [P, 1])
        gb_row = sb("gb_row", [1, E])
        ones_row = sb("ones_row", [1, P])
        gb = sb("gb", [P, E])
        pairsel = sb("pairsel", [96, EP, P], F32R)
        repeat = sb("repeat", [P, 4, P], F32R)
        vn_hi = sb("vn_hi", [P, CH], F32R)
        vn_lo = sb("vn_lo", [P, CH], F32R)
        half = sb("half", [P, NT])
        ones16 = sb("ones16", [P, BLK], F16)
        xin = sb("xin", [P, NT, D])
        xres = sb("xres", [P, NT, D])
        xn = sb("xn", [P, NT, D])
        st6 = sb("st6", [P, NT, 6])
        mv = sb("mv", [P, NT, 2])
        ve = sb("ve", [P, NT])
        y0 = sb("y0", [P, NT])
        nw = sb("nw", [P, NT])
        rstd = sb("rstd", [P, NT])
        xT = sb("xT", [P, S])
        xh = sb("xh", [P, S], F32R)
        xl = sb("xl", [P, S], F32R)
        qkh = sb("qkh", [P, 2, S], F16)
        qkl = sb("qkl", [P, 2, S], F16)
        vbd = sb("vbd", [P, NBLK, HG, 2 * BLK])
        nblk_r = -(-(nfr + nbf) // (HG * 2 * BLK))
        kr = vbd[:, 0:nblk_r].rearrange("p j g c -> p (j g c)")[:, 0:nfr + nbf]
        qtmp = sb("qtmp", [P, S], F16)
        qpad = sb("qpad", [P, NBLK, 4, BLK], F16)
        qall = sb("qall", [P, 2, S], F16)
        kall = sb("kall", [P, 2, S], F16)
        kpad = sb("kpad", [P, 2, NBLK, 4, BLK], F16)
        mxp = sb("mxp", [P, 2, NBLK])
        maxd = sb("maxd", [P, NBLK, BLK], F16)
        prob = stage[:].rearrange("p k t m -> p (k t m)")[:, 0:NPROB * CH].rearrange("p (n q) -> p n q", n=NPROB)
        ctxT = sb("ctxT", [P, S])
        qkf = [ctxT[:], prob[:, 0:S // CH, :].rearrange("p n q -> p (n q)")]
        sT = sb("sT", [P, S])
        th = sb("th", [P, NT, E])
        sc = sb("sc", [P, NT, E])
        sfc = sb("sfc", [P, NT, E])
        pm = sb("pm", [P, 4, NT, NGRP, 2])
        g2 = sb("g2", [P, 2, NT, NGRP])
        gs = sb("gs", [P, NT, NGRP])
        cmp_ = sb("cmp", [P, 2, NT, NGRP, NGRP])
        cnt = sb("cnt", [P, NT, NGRP])
        gm = sb("gm", [P, 2, NT, NGRP])
        msk = sb("msk", [P, NT, E])
        top = sb("top", [P, NT, 8])
        gt = sb("gt", [P, NT, E])
        eq = sb("eq", [P, NT, E])
        pre = sb("pre", [P, 2, NT, 2 * E])
        need = sb("need", [P, NT])
        cw = sb("cw", [P, NT, E])
        wsum = sb("wsum", [P, NT])
        cwT = sb("cwT", [96, S], F32R)
        k96 = xn[0:96].rearrange("p t d -> p (t d)")
        sg = sb("sg", [P, NHID, CH])
        a1 = sb("a1", [P, NHID, CH])
        a2 = sb("a2", [P, NHID, CH])
        z = sb("z", [P, S])
        rden = z[:, 0:CH]
        ot = sb("ot", [P, NT, D])

        filled = [sem(f"bank{i}_filled") for i in range(WORK + 2)]
        emptied = [sem(f"bank{i}_emptied") for i in range(WORK + 2)]
        consts_loaded = sem("consts_loaded")
        weights_loaded = sem("weights_loaded")
        small_ready = sem("small_ready")
        x_loaded = sem("x_loaded")
        xres_loaded = sem("xres_loaded")
        var_ready = sem("var_ready")
        pow_ready = sem("pow_ready")
        xn_ready = sem("xn_ready")
        xh_ready = sem("xh_ready")
        xl_ready = sem("xl_ready")
        lo_ready = sem("lo_ready")
        cw_ready = sem("cw_ready")
        qpad_ready = sem("qpad_ready")
        kpad_ready = sem("kpad_ready")
        max_ready = sem("max_ready")
        maxd_ready = sem("maxd_ready")
        pv_done = sem("pv_done")
        silu_ready = sem("silu_ready")
        down_done = sem("down_done")
        g_ready = sem("g_ready")
        o_ready = sem("o_ready")
        stored = [sem(f"stored{c}") for c in range(NCH)]

        x_v = x.rearrange("b (t p) d -> b p t d", p=P)
        out_v = out.rearrange("b (t p) d -> b p t d", p=P)

        def chunk(c):
            return slice(CH * c, CH * (c + 1))

        def sections(eng, walk):
            walk(At(FIRST, 0))
            with eng.Fori(0, B - 1) as b:
                walk(At(BODY, b))
            walk(At(LAST, B - 1))

        block = ctx.enter_context(nc.Block())

        @block.sync
        def _(sp):
            sp.dma_start(k32[:], c32).then_inc(consts_loaded, 16)
            sp.dma_start(xin[:], x_v[0]).then_inc(x_loaded, 16)
            sp.dma_start(kr, cr).then_inc(consts_loaded, 16)
            sp.dma_start(k16[:], c16).then_inc(consts_loaded, 16)
            for k, (w, ws) in enumerate(((Wg, Ws_g), (Wu, Ws_u))):
                sp.dma_start(stage[:, k, 0:EP, :], w.rearrange("(t e) i h -> (e i) t h", e=2)).then_inc(weights_loaded, 16)
                sp.dma_start(stage[:, k, EP, :], ws).then_inc(weights_loaded, 16)
            sp.dma_start(stage[:, 2, 0:EP, :].rearrange("h t (e i) -> h (t e) i", e=2),
                         Wd.rearrange("e h i -> h e i")).then_inc(weights_loaded, 16)
            sp.dma_start(stage[:, 2, EP, :], Ws_d).then_inc(weights_loaded, 16)
            sp.dma_start(wqkv[:], w_qkv).then_inc(weights_loaded, 16)
            sp.dma_start(wout[:], w_out).then_inc(weights_loaded, 16)
            sp.dma_start(gate_nat[:], gate_w).then_inc(weights_loaded, 16)
            for k in range(3):
                sp.dma_start(bias3[:, k:k + 1], b_qkv[D * k:D * (k + 1)].rearrange("(p a) -> p a", a=1))\
                    .then_inc(weights_loaded, 16)
            sp.dma_start(bo[:], b_out.rearrange("(p a) -> p a", a=1)).then_inc(weights_loaded, 16)
            sp.dma_start(gb_row[:], gate_bias.rearrange("(a e) -> a e", a=1)).then_inc(weights_loaded, 16)
            sp.dma_start(xres[:], x_v[0]).then_inc(xres_loaded, 16)

            def store(at, c):
                sp.wait_ge(emptied[at.bank(("outT", c))], at.taken(("outT", c)))
                sp.dma_start(out_v[at.b, :, TPC * c:TPC * (c + 1), :] if isinstance(at.b, int) else
                             out_v[bass.ds(at.b, 1), :, TPC * c:TPC * (c + 1), :].rearrange("a p t d -> p (a t) d"),
                             ot[:, TPC * c:TPC * (c + 1), :]).then_inc(stored[c], 16)

            with sp.Fori(0, B - 1) as b:
                at = At(BODY, b)
                sp.wait_ge(xn_ready, NCH * b + NCH)
                sp.dma_start(xin[:], x_v[bass.ds(b + 1, 1)].rearrange("a p t d -> p (a t) d")).then_inc(x_loaded, 16)
                for c in range(NCH):
                    store(at, c)
                sp.dma_start(xres[:], x_v[bass.ds(b + 1, 1)].rearrange("a p t d -> p (a t) d")).then_inc(xres_loaded, 16)
            for c in range(NCH):
                store(At(LAST, B - 1), c)
            for c in range(NCH):
                sp.wait_ge(stored[c], 16 * (B + 1))

        @block.tensor
        def _(pe):
            def fill(at, tile):
                pe.wait_ge(emptied[at.bank(tile)], at.free(tile))
                return banks[at.bank(tile)]

            def done(at, tile, ins):
                ins.then_inc(filled[at.bank(tile)], 1)

            def parts3(ps, w_hi, w_lo, c):
                pe.matmul(ps[:], w_hi, xh[:, chunk(c)], start=True, stop=False)
                pe.matmul(ps[:], w_lo, xh[:, chunk(c)], start=False, stop=False)
                return pe.matmul(ps[:], w_hi, xl[:, chunk(c)], start=False, stop=True)

            def walk(at):
                b, opened = at.b, set()
                for s in at.steps:
                    kind = s[0]
                    if kind == "weights":
                        if s[1] == 0 and s[2] == 0:
                            pe.wait_ge(consts_loaded, 48)
                            pe.wait_ge(weights_loaded, 14 * 16)
                        ps = fill(at, s)
                        for i in range(s[2], s[3]):
                            ins = pe.transpose(ps[:, P * (i - s[2]):P * (i - s[2] + 1)], stage[:, s[1], i, :], ident)
                        done(at, s, ins)
                    elif kind == "small":
                        pe.wait_ge(small_ready, 1)
                        ps = fill(at, s)
                        pe.transpose(ps[:, 0:E], gate_nat[:], ident[0:E, 0:E])
                        pe.matmul(ps[:, 32:32 + E], ones_row[:], gb_row[:], start=True, stop=True)
                        done(at, s, pe.matmul(ps[:, 64:65], wout[:], bias3[:, 2:3], start=True, stop=True))
                    elif kind == "xT":
                        c = s[1]
                        pe.wait_ge(xn_ready, at.next * NCH + (c + 1))
                        ps = fill(at, s)
                        for i in range(TPC):
                            ins = pe.transpose(ps[:, P * i:P * (i + 1)], xn[:, TPC * c + i, :], ident)
                        done(at, s, ins)
                    elif kind in ("q", "k"):
                        c, w = s[1], "qk".index(kind)
                        if kind == "q":
                            pe.wait_ge(xl_ready, at.next * NCH + (c + 1))
                            if at.section is FIRST and c == 0:
                                pe.wait_ge(small_ready, 2)
                        ps = fill(at, s)
                        done(at, s, parts3(ps, wqk_hi[:, D * w:D * (w + 1)], wqk_lo[:, D * w:D * (w + 1)], c))
                    elif kind == "vn":
                        c = s[1]
                        pe.wait_ge(emptied[at.bank(("xT", c))], at.taken(("xT", c)))
                        ps = fill(at, s)
                        for i in range(TPC):
                            ins = pe.matmul(ps[:, D * i:D * (i + 1)], xT[:, CH * c + P * i:CH * c + P * (i + 1)],
                                            wqkv[:, 2 * D:3 * D], start=True, stop=True)
                        done(at, s, ins)
                    elif kind == "v":
                        c, i = s[1], s[2]
                        if i == 0:
                            pe.wait_ge(emptied[at.bank(("vn", c))], at.taken(("vn", c)))
                        ps = fill(at, s)
                        pe.matmul(ps[:], repeat[:, i, :], vn_hi[:], start=True, stop=False)
                        done(at, s, pe.matmul(ps[:], repeat[:, i, :], vn_lo[:], start=False, stop=True))
                    elif kind == "gate":
                        ps = fill(at, s)
                        for t in range(NT):
                            ins = pe.matmul(ps[:, E * t:E * (t + 1)], xT[:, P * t:P * (t + 1)], gateT[:],
                                            start=True, stop=True)
                        done(at, s, ins)
                    elif kind == "cwT":
                        c = s[1]
                        pe.wait_ge(cw_ready, b + 1)
                        ps = fill(at, s)
                        for i in range(TPC):
                            ins = pe.transpose(ps[0:E, P * i:P * (i + 1)], cw[:, TPC * c + i, :], ident)
                        done(at, s, ins)
                    elif kind in ("qsel", "ksel", "qfull"):
                        g, c = s[1], s[2]
                        w = 1 if kind == "ksel" else 0
                        if g == 0 and c == 0:
                            pe.wait_ge(lo_ready, b * 2 * NCH + 2 * NCH)
                        if kind == "qfull" and c == 0:
                            pe.wait_ge(maxd_ready, b * HG + (g + 1))
                        ps = fill(at, s)
                        n = "qk"[w]
                        pe.matmul(ps[:], const16(n + "_a", g), qkh[:, w, chunk(c)], start=True, stop=False)
                        ins = pe.matmul(ps[:], const16(n + "_b", g), qkl[:, w, chunk(c)], start=False,
                                        stop=(kind != "qfull"))
                        if kind == "qfull":
                            ins = pe.matmul(ps[:], const16("negmax"), maxd[:, BPC * c:BPC * (c + 1), :],
                                            start=False, stop=True)
                        done(at, s, ins)
                    elif kind == "max":
                        g, n = s[1], s[2]
                        if n == 0:
                            pe.wait_ge(qpad_ready, b * HG + (g + 1))
                            for c in range(NCH):
                                pe.wait_ge(emptied[at.bank(("ksel", g, c))], at.taken(("ksel", g, c)))
                        ps = fill(at, s)
                        if g == 0:
                            j, c, cols = GM[n]
                            last = CH * c + cols == BLK * (j + 1)
                            ins = pe.matmul(ps[:, 0:cols], qpad[:, j, :, :], kall[:, g % 2, CH * c:CH * c + cols],
                                            start=True, stop=not last, skip_group_check=True)
                            if last:
                                ins = pe.matmul(ps[:, cols - BLK:cols], constbf("identb"), constbf("win")[:, BLK:2 * BLK],
                                                start=False, stop=True, skip_group_check=True)
                        else:
                            pe.matmul(ps[:], constbf("identb"), constbf("win0" if n == 0 else "win"), start=True, stop=False,
                                      skip_group_check=True)
                            for i in range(LOC):
                                j = LOC * n + i
                                lo = max(0, BLK * (j - 1))
                                cols = BLK * (j + 1) - lo
                                ins = pe.matmul(ps[:, 2 * BLK * (i + 1) - cols:2 * BLK * (i + 1)], qpad[:, j, :, :],
                                                kall[:, g % 2, lo:lo + cols], start=False, stop=(i == LOC - 1),
                                                skip_group_check=True)
                        done(at, s, ins)
                    elif kind == "score":
                        g, n = s[1], s[2]
                        if n == 0:
                            for c in range(NCH):
                                pe.wait_ge(emptied[at.bank(("qfull", g, c))], at.taken(("qfull", g, c)))
                            pe.wait_ge(kpad_ready, b * HG + (g + 1))
                        ps = fill(at, s)
                        if g == 0:
                            j, c, q0, cols = GT[n]
                            diag = q0 == BLK * j
                            ins = pe.matmul(ps[:, 0:cols], kpad[:, g % 2, j, :, :], qall[:, g % 2, q0:q0 + cols],
                                            start=True, stop=not diag, skip_group_check=True)
                            if diag:
                                ins = pe.matmul(ps[:, 0:BLK], constbf("identb"), constbf("win")[:, 0:BLK],
                                                start=False, stop=True, skip_group_check=True)
                        else:
                            pe.matmul(ps[:], constbf("identb"), constbf("win"), start=True, stop=False,
                                      skip_group_check=True)
                            for i in range(LOC):
                                j = LOC * n + i
                                cols = min(2 * BLK, S - BLK * j)
                                ins = pe.matmul(ps[:, 2 * BLK * i:2 * BLK * i + cols], kpad[:, g % 2, j, :, :],
                                                qall[:, g % 2, BLK * j:BLK * j + cols], start=False, stop=(i == LOC - 1),
                                                skip_group_check=True)
                        done(at, s, ins)
                    elif kind == "pv":
                        g, n = s[1], s[2]
                        t = SCORES_BEFORE[g] + n
                        if n == 0:
                            fill(at, ("acc", g))
                            opened = set()
                        acc = banks[at.bank(("acc", g))]
                        tile = ("score", g, n)
                        pe.wait_ge(emptied[at.bank(tile)], at.taken(tile))
                        pieces = []
                        if g == 0:
                            j, c, q0, cols = GT[n]
                            spans = [(j, q0, 0, cols)]
                        else:
                            spans = [(j, BLK * j, 2 * BLK * (j - LOC * n), min(2 * BLK, S - BLK * j))
                                     for j in range(LOC * n, LOC * (n + 1))]
                        for j, q0, col, cols in spans:
                            q = q0
                            while q < q0 + cols:
                                to = min(q0 + cols, (q // QTR + 1) * QTR)
                                pieces.append((j, q // QTR, q, col + q - q0, to - q))
                                q = to
                        for j, qt, q, col, cols in pieces:
                            r, o = 64 * (qt % 2), QTR * (qt // 2) + q % QTR
                            ins = pe.matmul(acc[r:r + 64, o:o + cols], vbd[:, j, g, :], prob[:, t % NPROB, col:col + cols],
                                            start=r not in opened, stop=False, skip_group_check=True)
                            opened.add(r)
                        ins.then_inc(pv_done, 1)
                    elif kind == "proj":
                        c = s[1]
                        if c == 0:
                            for g in (HG - 2, HG - 1):
                                pe.wait_ge(emptied[at.bank(("acc", g))], at.taken(("acc", g)))
                        ps = fill(at, s)
                        done(at, s, pe.matmul(ps[:], wout[:], ctxT[:, chunk(c)], start=True, stop=True))
                    elif kind == "up":
                        c, t = s[1], s[2]
                        for w, part in enumerate(("gate", "up")):
                            ps = fill(at, s + (part,))
                            done(at, s + (part,), parts3(ps, up_hi[:, w, t, :], up_lo[:, w, t, :], c))
                        if t < EP:
                            if t == 0:
                                pe.wait_ge(emptied[at.bank(("cwT", c))], at.taken(("cwT", c)))
                            ps = fill(at, s + ("weight",))
                            done(at, s + ("weight",), pe.matmul(ps[:], pairsel[:, t, :], cwT[:, chunk(c)],
                                                                start=True, stop=True))
                    elif kind == "down":
                        c, t = s[1], s[2]
                        i = NUP * c + t
                        if t == 0:
                            fill(at, ("y", c))
                        tile = ("up", c, t, "weight" if t < EP else "up")
                        pe.wait_ge(emptied[at.bank(tile)], at.taken(tile))
                        pe.matmul(banks[at.bank(("y", c))][:], down_w[:, t, :], a2[:, i % NHID, :],
                                  start=(t == 0), stop=(t == NUP - 1)).then_inc(down_done, 1)
                    elif kind == "outT":
                        c = s[1]
                        pe.wait_ge(o_ready, b * NCH + (c + 1))
                        ps = fill(at, s)
                        for i in range(TPC):
                            ins = pe.transpose(ps[:, P * i:P * (i + 1)], sT[:, CH * c + P * i:CH * c + P * (i + 1)], ident)
                        done(at, s, ins)

            sections(pe, walk)

        @block.scalar
        def _(act):
            def walk(at):
                b = at.b
                if at.section is FIRST:
                    act.wait_ge(consts_loaded, 48)
                    act.wait_ge(small_ready, 3)
                for s in at.steps:
                    kind = s[0]
                    if kind == "up":
                        tile = s + ("gate",)
                        i = NUP * s[1] + s[2]
                        act.wait_ge(filled[at.bank(tile)], at.filled(tile))
                        if i >= NHID:
                            old = ("up", (i - NHID) // NUP, (i - NHID) % NUP, "up")
                            act.wait_ge(emptied[at.bank(old)], at.taken(old))
                        act.activation(sg[:, i % NHID, :], banks[at.bank(tile)][:], ACT.Silu).then_inc(emptied[at.bank(tile)], 1)
                        continue
                    if kind == "z":
                        c = s[1]
                        act.wait_ge(emptied[at.bank(("y", c))], at.taken(("y", c)))
                        act.activation(z[:, chunk(c)], z[:, chunk(c)], ACT.Silu).then_inc(g_ready, 1)
                        continue
                    if kind not in ("xT", "q", "k", "gate", "qsel", "ksel", "qfull", "score", "proj"):
                        continue
                    ps, freed = banks[at.bank(s)], emptied[at.bank(s)]
                    act.wait_ge(filled[at.bank(s)], at.filled(s))
                    if kind == "xT":
                        act.activation(xT[:, chunk(s[1])], ps[:], ACT.Copy).then_inc(freed, 1)
                    elif kind in ("q", "k"):
                        w, c = "qk".index(kind), s[1]
                        scale, bias = (Q_SCALE, bq[:]) if kind == "q" else (1.0, bias3[:, 1:2])
                        act.activation(qkf[w][:, chunk(c)], ps[:], ACT.Identity, bias=bias, scale=scale)
                        act.activation(qkh[:, w, chunk(c)], ps[:], ACT.Identity, bias=bias, scale=scale).then_inc(freed, 1)
                    elif kind == "gate":
                        act.activation(th[:].rearrange("p t e -> p (t e)"), ps[:, 0:NT * E], ACT.Tanh, scale=0.5)\
                            .then_inc(freed, 1)
                    elif kind == "qsel":
                        act.activation(qtmp[:, chunk(s[2])], ps[:], ACT.Copy).then_inc(freed, 1)
                    elif kind == "ksel":
                        act.activation(kall[:, s[1] % 2, chunk(s[2])], ps[:], ACT.Identity, bias=const32("onerow"))\
                            .then_inc(freed, 1)
                    elif kind == "qfull":
                        act.activation(qall[:, s[1] % 2, chunk(s[2])], ps[:], ACT.Copy).then_inc(freed, 1)
                    elif kind == "score":
                        g, n = s[1], s[2]
                        t = SCORES_BEFORE[g] + n
                        cols = GT[n][3] if g == 0 else CH
                        if t >= NPROB:
                            act.wait_ge(pv_done, b * SCORES_BEFORE[HG] + (t - NPROB + 1))
                        act.activation(prob[:, t % NPROB, 0:cols], ps[:, 0:cols], ACT.Exp).then_inc(freed, 1)
                    elif kind == "proj":
                        act.activation(sT[:, chunk(s[1])], ps[:], ACT.Identity, bias=bs[:]).then_inc(freed, 1)

            sections(act, walk)

        @block.vector
        def _(dve):
            def setup():
                for r in emptied:
                    dve.sem_inc(r, 1)
                for st in stored:
                    dve.sem_inc(st, 16)
                dve.memset(ones_row[:], 1.0).then_inc(small_ready, 1)
                dve.memset(qpad[:], 0.0)
                dve.memset(kpad[:], 0.0)
                dve.memset(pre[:], 0.0)
                dve.memset(k96, 0.0)
                dve.wait_ge(consts_loaded, 48)
                dve.wait_ge(weights_loaded, 14 * 16)
                dve.drain()
                dve.tensor_copy(cwT[:], k96)
                dve.tensor_copy(pairsel[:].rearrange("p t m -> p (t m)"), kr[0:96, frat["pairsel"][0]:frat["pairsel"][1]])
                dve.tensor_copy(kbf[:], kr[:, nfr:nfr + nbf])
                dve.tensor_copy(repeat[:].rearrange("p i m -> p (i m)"), kr[:, frat["repeat"][0]:frat["repeat"][1]])
                dve.drain()
                dve.tensor_copy(vbd[:, :, :, BLK:2 * BLK].rearrange("p j g c -> p j (g) c"),
                                vmask.unsqueeze(1).broadcast_to([P, NBLK, HG, BLK]))
                dve.tensor_scalar(bq[:], bias3[:, 0:1], Q_SCALE, None, ALU.mult)
                dve.tensor_copy(wqk_hi[:], wqkv[:, 0:2 * D])
                dve.drain()
                dve.tensor_tensor(wqk_lo[:], wqkv[:, 0:2 * D], wqk_hi[:].bitcast(F32), ALU.subtract)\
                    .then_inc(small_ready, 2)

            def tt(out_, a, b_, op):
                return dve.tensor_tensor(out_, a, b_, op)

            def ts(out_, a, s1, s2, op0, op1=None):
                return dve.tensor_scalar(out_, a, s1, s2, op0, op1) if op1 else dve.tensor_scalar(out_, a, s1, s2, op0)

            def routing():
                def over(a, shape, axis):
                    return a.unsqueeze(axis).broadcast_to(shape)

                NG = [P, NT, NGRP, NGRP]
                ts(sc[:], th[:], 0.5, 0.5, ALU.mult, ALU.add)
                dve.drain()
                tt(sfc[:], sc[:], over(gb[:], [P, NT, E], 1), ALU.add)
                dve.drain()
                pairs = sfc[:].rearrange("p t (g a b) -> p (t g) a b", g=NGRP, a=2)
                hi2, lo2 = (pm[:, i].rearrange("p t g a -> p (t g) a") for i in range(2))
                tt(hi2, pairs[:, :, :, 0], pairs[:, :, :, 1], ALU.max)
                tt(lo2, pairs[:, :, :, 0], pairs[:, :, :, 1], ALU.min)
                dve.drain()
                flat = [pm[:, i].rearrange("p t g a -> p (t g) a") for i in range(4)]
                g2f = [g2[:, i].rearrange("p t g -> p (t g)") for i in range(2)]
                tt(g2f[0], flat[0][:, :, 0], flat[0][:, :, 1], ALU.max)
                tt(flat[2][:, :, 0], flat[0][:, :, 0], flat[0][:, :, 1], ALU.min)
                tt(flat[2][:, :, 1], flat[1][:, :, 0], flat[1][:, :, 1], ALU.max)
                dve.drain()
                tt(g2f[1], flat[2][:, :, 0], flat[2][:, :, 1], ALU.max)
                dve.drain()
                tt(gs[:], g2[:, 0], g2[:, 1], ALU.add)
                dve.drain()
                other, own = over(gs[:], NG, 2), over(gs[:], NG, 3)
                tt(cmp_[:, 0], other, own, ALU.is_gt)
                tt(cmp_[:, 1], other, own, ALU.is_ge)
                dve.drain()
                tt(cmp_[:, 1], cmp_[:, 1], cmp_[:, 0], ALU.subtract)
                dve.drain()
                lower = const32("lower").rearrange("p (i j) -> p i j", i=NGRP)
                tt(cmp_[:, 1], cmp_[:, 1], over(lower, NG, 1), ALU.mult)
                dve.drain()
                tt(cmp_[:, 0], cmp_[:, 0], cmp_[:, 1], ALU.add)
                dve.drain()
                dve.tensor_reduce(cnt[:], cmp_[:, 0], AX_X, ALU.add)
                dve.drain()
                ts(gm[:, 0], cnt[:], float(TOPG), None, ALU.is_lt)
                ts(gm[:, 1], cnt[:], float(TOPG), -1e30, ALU.is_ge, ALU.mult)
                dve.drain()
                of_group = "p t (g e) -> p t g e"
                tt(msk[:].rearrange(of_group, g=NGRP), sfc[:].rearrange(of_group, g=NGRP), over(gm[:, 0], NG, 3), ALU.mult)
                dve.drain()
                tt(msk[:].rearrange(of_group, g=NGRP), msk[:].rearrange(of_group, g=NGRP), over(gm[:, 1], NG, 3), ALU.add)
                dve.drain()
                for t in range(NT):
                    dve.max(top[:, t, :], msk[:, t, :])
                dve.drain()
                kth = top[:, :, TOPK - 1:TOPK].broadcast_to([P, NT, E])
                tt(gt[:], msk[:], kth, ALU.is_gt)
                tt(eq[:], msk[:], kth, ALU.is_equal)
                tt(pre[:, 0, :, E:2 * E], msk[:], kth, ALU.is_equal)
                dve.drain()
                dve.tensor_reduce(need[:], gt[:], AX_X, ALU.add)
                src = 0
                for sh in (1, 2, 4, 8):
                    tt(pre[:, 1 - src, :, E:2 * E], pre[:, src, :, E:2 * E], pre[:, src, :, E - sh:2 * E - sh], ALU.add)
                    dve.drain()
                    src = 1 - src
                run = pre[:, src, :, E:2 * E]
                tt(run, run, over(need[:], [P, NT, E], 2), ALU.add)
                dve.drain()
                ts(run, run, float(TOPK), None, ALU.is_le)
                dve.drain()
                tt(eq[:], eq[:], run, ALU.mult)
                dve.drain()
                tt(gt[:], gt[:], eq[:], ALU.add)
                dve.drain()
                tt(msk[:], sc[:], gt[:], ALU.mult)
                dve.drain()
                dve.tensor_reduce(need[:], msk[:], AX_X, ALU.add)
                dve.drain()
                ts(need[:], need[:], 1e-20, None, ALU.add)
                dve.drain()
                dve.reciprocal(wsum[:], need[:])
                dve.drain()
                dve.scalar_tensor_tensor(out=cw[:], in0=msk[:], scalar=ROUTE_SCALE, in1=over(wsum[:], [P, NT, E], 2),
                                         op0=ALU.mult, op1=ALU.mult).then_inc(cw_ready, 1)

            def weigh(at, c, t):
                i = NUP * c + t
                tile, up = ("up", c, t, "weight"), ("up", c, t, "up")
                dve.wait_ge(emptied[at.bank(up)], at.taken(up))
                dve.wait_ge(filled[at.bank(tile)], at.filled(tile))
                if i >= NHID:
                    dve.wait_ge(down_done, at.b * NCH * NUP + (i - NHID + 1))
                tt(a2[:, i % NHID, :], a1[:, i % NHID, :], banks[at.bank(tile)][:], ALU.mult)\
                    .then_inc(emptied[at.bank(tile)], 1)

            def walk(at):
                b = at.b
                if at.section is FIRST:
                    setup()
                for s in at.steps:
                    kind = s[0]
                    if kind == "stats":
                        dve.wait_ge(x_loaded, at.next * 16 + 16)
                        for t in range(NT):
                            dve.bn_stats(st6[:, t, :], xin[:, t, :])
                        dve.drain()
                        for t in range(NT):
                            dve.bn_aggr(mv[:, t, :], st6[:, t, :])
                        dve.drain()
                        ts(ve[:], mv[:, :, 1], LN_EPS, None, ALU.add).then_inc(var_ready, 1)
                    elif kind == "ln":
                        c = s[1]
                        if c == 0:
                            dve.wait_ge(pow_ready, at.next + 1)
                            tt(nw[:], y0[:], y0[:], ALU.mult)
                            dve.drain()
                            tt(nw[:], nw[:], ve[:], ALU.mult)
                            dve.drain()
                            ts(nw[:], nw[:], -0.5, 1.5, ALU.mult, ALU.add)
                            dve.drain()
                            tt(rstd[:], y0[:], nw[:], ALU.mult)
                            dve.drain()
                        for t in range(TPC * c, TPC * (c + 1)):
                            ins = ts(xn[:, t, :], xin[:, t, :], mv[:, t, 0:1], rstd[:, t:t + 1], ALU.subtract, ALU.mult)
                        ins.then_inc(xn_ready, 1)
                    elif kind == "xT":
                        dve.wait_ge(emptied[at.bank(s)], at.taken(s))
                        dve.tensor_copy(xh[:, chunk(s[1])], xT[:, chunk(s[1])]).then_inc(xh_ready, 1)
                    elif kind == "pads":
                        g = s[1]
                        for c in range(NCH):
                            dve.wait_ge(emptied[at.bank(("qsel", g, c))], at.taken(("qsel", g, c)))
                        for h in range(4):
                            r = slice(32 * h, 32 * h + 32)
                            ins = dve.tensor_copy(qpad[r, :, h, :], qtmp[r, :].rearrange("p (j q) -> p j q", q=BLK))
                        ins.then_inc(qpad_ready, 1)
                    elif kind == "maxdone" and s[1] == 0:
                        dve.drain()
                        tt(mxp[:, 0, BPC:NBLK], mxp[:, 0, BPC:NBLK], mxp[:, 1, BPC:NBLK], ALU.max).then_inc(max_ready, 1)
                    elif kind == "gate":
                        dve.wait_ge(emptied[at.bank(s)], at.taken(s))
                        routing()
                    elif kind == "norm":
                        g = s[1]
                        bank = at.bank(("acc", g))
                        dve.drain()
                        dve.wait_ge(pv_done, b * SCORES_BEFORE[HG] + SCORES_BEFORE[g + 1])
                        dve.reciprocal(rden, banks[bank][:])
                        dve.drain()
                        for u in range(2):
                            ins = tt(ctxT[32 * g:32 * g + 32, :].rearrange("p (v u q) -> p u v q", u=2, q=QTR)[:, u],
                                     banks[bank][64 * u:64 * u + 32, :].rearrange("p (v q) -> p v q", q=QTR),
                                     rden[64 * u + 32:64 * u + 64, :].rearrange("p (v q) -> p v q", q=QTR), ALU.mult)
                        ins.then_inc(emptied[bank], 1)
                    elif kind == "z":
                        c = s[1]
                        bank = at.bank(("y", c))
                        dve.wait_ge(down_done, b * NCH * NUP + NUP * (c + 1))
                        tt(z[:, chunk(c)], xT[:, chunk(c)], banks[bank][:], ALU.add).then_inc(emptied[bank], 1)
                    elif kind == "up":
                        c, t = s[1], s[2]
                        i = NUP * c + t
                        gate, up = s + ("gate",), s + ("up",)
                        dve.wait_ge(emptied[at.bank(gate)], at.taken(gate))
                        dve.wait_ge(filled[at.bank(up)], at.filled(up))
                        if t == EP and i >= NHID:
                            dve.wait_ge(down_done, b * NCH * NUP + (i - NHID + 1))
                        tt((a1 if t < EP else a2)[:, i % NHID, :], sg[:, i % NHID, :], banks[at.bank(up)][:], ALU.mult)\
                            .then_inc(emptied[at.bank(up)], 1)
                        if t > 0:
                            weigh(at, c, t - 1)
                    elif kind in ("weights", "small", "vn", "v", "cwT", "max", "outT"):
                        ps, freed = banks[at.bank(s)], emptied[at.bank(s)]
                        dve.wait_ge(filled[at.bank(s)], at.filled(s))
                        if kind == "weights":
                            k, lo, hi = s[1], s[2], s[3]
                            tile = ps[:, 0:P * (hi - lo)].rearrange("p (t m) -> p t m", m=P)
                            if k == 2:
                                dve.tensor_copy(down_w[:, lo:hi, :], tile).then_inc(freed, 1)
                            else:
                                dve.tensor_copy(up_hi[:, k, lo:hi, :], tile)
                                dve.drain()
                                tt(up_lo[:, k, lo:hi, :], tile, up_hi[:, k, lo:hi, :].bitcast(F32), ALU.subtract).then_inc(freed, 1)
                        elif kind == "small":
                            dve.tensor_copy(gateT[:], ps[:, 0:E])
                            dve.tensor_copy(gb[:], ps[:, 32:32 + E])
                            tt(bs[:], bo[:], ps[:, 64:65], ALU.add).then_inc(freed, 1)
                        elif kind == "vn":
                            dve.tensor_copy(vn_hi[:], ps[:])
                            dve.drain()
                            tt(vn_lo[:], ps[:], vn_hi[:].bitcast(F32), ALU.subtract).then_inc(freed, 1)
                        elif kind == "v":
                            c, i = s[1], s[2]
                            tt(vbd[:].rearrange("p (t i) g c -> p i t g c", i=4)[:, i, TPC * c:TPC * (c + 1), :, 0:BLK],
                               ps[:].rearrange("p (j g c) -> p j g c", j=4, g=HG),
                               vmask.unsqueeze(1).broadcast_to([P, 4, HG, BLK]), ALU.mult).then_inc(freed, 1)
                        elif kind == "cwT":
                            c = s[1]
                            dve.tensor_copy(cwT[0:E, chunk(c)], ps[0:E, :])
                            dve.drain()
                            tt(cwT[32:32 + E, chunk(c)], ps[0:E, :], cwT[0:E, chunk(c)].bitcast(F32), ALU.subtract).then_inc(freed, 1)
                        elif kind == "max":
                            g, n = s[1], s[2]
                            if g == 0:
                                j, c, cols = GM[n]
                                ins = dve.tensor_reduce(mxp[:, c, j:j + 1], ps[:, 0:cols], AX_X, ALU.max)
                            else:
                                ins = dve.tensor_reduce(mxp[:, 0, LOC * n:LOC * (n + 1)],
                                                        ps[:].rearrange("p (j q) -> p j q", q=2 * BLK), AX_X, ALU.max)
                            ins.then_inc(freed, 1)
                        elif kind == "outT":
                            c = s[1]
                            dve.wait_ge(xres_loaded, b * 16 + 16)
                            dve.wait_ge(stored[c], b * 16 + 16)
                            tt(ot[:, TPC * c:TPC * (c + 1), :], xres[:, TPC * c:TPC * (c + 1), :],
                               ps[:].rearrange("p (t d) -> p t d", d=D), ALU.add).then_inc(freed, 1)

            sections(dve, walk)

        @block.gpsimd
        def _(pool):
            def walk(at):
                b = at.b
                if at.section is FIRST:
                    pool.memset(half[:], -0.5)
                    pool.memset(ones16[:], 1.0)
                    pool.wait_ge(small_ready, 3)
                    pool.drain()
                for s in at.steps:
                    kind = s[0]
                    if kind == "stats":
                        pool.wait_ge(var_ready, at.next + 1)
                        pool.tensor_tensor(y0[:], ve[:], half[:], ALU.pow).then_inc(pow_ready, 1)
                    elif kind == "xT":
                        c = s[1]
                        pool.wait_ge(xh_ready, at.next * NCH + (c + 1))
                        pool.tensor_tensor(xl[:, chunk(c)], xT[:, chunk(c)], xh[:, chunk(c)].bitcast(F32), ALU.subtract)\
                            .then_inc(xl_ready, 1)
                    elif kind in ("q", "k"):
                        w, c = "qk".index(kind), s[1]
                        pool.wait_ge(emptied[at.bank(s)], at.taken(s))
                        pool.tensor_tensor(qkl[:, w, chunk(c)], qkf[w][:, chunk(c)], qkh[:, w, chunk(c)], ALU.subtract)\
                            .then_inc(lo_ready, 1)
                    elif kind == "pads":
                        g = s[1]
                        for c in range(NCH):
                            pool.wait_ge(emptied[at.bank(("ksel", g, c))], at.taken(("ksel", g, c)))
                        for h in range(4):
                            r = slice(32 * h, 32 * h + 32)
                            keys = kall[r, g % 2, :].rearrange("p (j q) -> p j q", q=BLK)
                            if h == 0:
                                pool.tensor_tensor(kpad[r, g % 2, :, h, :], keys,
                                                   ones16[r].unsqueeze(1).broadcast_to([BLK, NBLK, BLK]), ALU.mult)
                            else:
                                ins = pool.tensor_copy(kpad[r, g % 2, :, h, :], keys)
                        ins.then_inc(kpad_ready, 1)
                        pool.drain()
                    elif kind == "maxdone":
                        g = s[1]
                        if g == 0:
                            pool.wait_ge(max_ready, b + 1)
                        else:
                            tile = ("max", g, MAXES[g] - 1)
                            pool.wait_ge(emptied[at.bank(tile)], at.taken(tile))
                        pool.tensor_tensor(maxd[:], mxp[:, 0, :].unsqueeze(2).broadcast_to([P, NBLK, BLK]),
                                           const32("eye32").unsqueeze(1).broadcast_to([P, NBLK, BLK]), ALU.mult)\
                            .then_inc(maxd_ready, 1)
                    elif kind == "z":
                        c = s[1]
                        pool.wait_ge(g_ready, b * NCH + (c + 1))
                        pool.wait_ge(emptied[at.bank(("proj", c))], at.taken(("proj", c)))
                        pool.tensor_tensor(sT[:, chunk(c)], sT[:, chunk(c)], z[:, chunk(c)], ALU.mult).then_inc(o_ready, 1)

            sections(pool, walk)


_INS = ["L0_attn_x", "L0_attn_w_qkv", "L0_attn_b_qkv", "L0_attn_w_out", "L0_attn_b_out", "L0_ffn_gate_w",
        "L0_ffn_gate_bias", "L0_ffn_Wg", "L0_ffn_Wu", "L0_ffn_Wd", "L0_ffn_Ws_g", "L0_ffn_Ws_u", "L0_ffn_Ws_d"]
_OUTS = [((B, S, D), "float32")]


def constants():
    import numpy as np

    rows, cols = np.arange(P)[:, None], np.arange(P)[None, :]
    head, r = rows // BLK, rows % BLK
    f32 = {
        "ident": rows == cols,
        "vmask": np.tile(head == np.arange(BLK)[None, :] // HD, (1, HG)),
        "eye32": r == np.arange(BLK)[None, :],
        "onerow": r == 3 * HD,
    }
    fr = {
        "pairsel": (rows % BLK == np.arange(EP * P)[None, :] // I) & (rows < 2 * BLK),
        "repeat": rows == BLK * (np.arange(4 * P)[None, :] // P) + np.arange(4 * P)[None, :] % BLK,
    }
    f32 |= {
        "lower": np.tile((np.arange(NGRP)[None, :] < np.arange(NGRP)[:, None]).reshape(1, -1), (P, 1)),
    }
    feature_head, dim = rows // HD, rows % HD

    def select(g, groups):
        out = np.zeros((P, P), bool)
        for part in groups:
            out |= cols == (feature_head - 4 * g) * BLK + part * HD + dim
        return out & (feature_head // 4 == g)

    f16 = {name: np.concatenate([select(g, groups) for g in range(HG)], 1)
           for name, groups in (("q_a", (0, 2)), ("q_b", (1,)), ("k_a", (0, 1)), ("k_b", (2,)))}
    f16["negmax"] = -1.0 * (cols == head * BLK + 3 * HD)
    c = np.arange(CH)[None, :]
    inside = (c % (2 * BLK) >= r) & (c % (2 * BLK) <= r + WINDOW)
    bf = {
        "identb": 1.0 * (rows == cols),
        "win": np.where(inside, 0.0, -1e30),
        "win0": np.where(inside & (c >= BLK), 0.0, -1e30),
    }

    def packed(parts, sizes, dtype):
        return np.concatenate([np.asarray(parts[n]).astype(dtype) for n in sizes], 1)

    return {"c32": packed(f32, C32, np.float32), "cr": packed(fr | bf, CR | CBF, np.float32),
            "c16": packed(f16, C16, np.float16)}


def kernel(**inputs):
    import numpy as _np
    import concourse.bacc as _bacc
    from concourse import mybir as _mybir
    from concourse.bass_utils import run_bass_kernel_spmd as _run

    nc = _bacc.Bacc("TRN2", target_bir_lowering=False, num_devices=1)
    arrays, args = {}, []
    for name, a in [(n, _np.ascontiguousarray(inputs[n])) for n in _INS] + list(constants().items()):
        arrays[f"in_{name}_dram"] = a
        args.append(nc.dram_tensor(f"in_{name}_dram", a.shape, _mybir.dt.from_np(a.dtype), kind="ExternalInput").ap())
    for i, (shape, dtype) in enumerate(_OUTS):
        dt = _mybir.dt.from_np(_np.dtype(dtype))
        args.append(nc.dram_tensor(f"out_{i}_dram", shape, dt, kind="ExternalOutput").ap())
    build(nc, *args)
    r = _run(nc, [arrays], core_ids=[0])
    got = tuple(r.results[0][f"out_{i}_dram"] for i in range(len(_OUTS)))
    return got[0]
```

```python
from contextlib import ExitStack

import concourse.bass as bass
from concourse import mybir

F32 = mybir.dt.float32
F32R = mybir.dt.float32r
F16 = mybir.dt.float16
BF16 = mybir.dt.bfloat16
ALU = mybir.AluOpType
ACT = mybir.ActivationFunctionType
AX_X = mybir.AxisListType.X

P = 128
B, S, D = 4, 1024, 128
H, HD = 16, 8
HG = H // 4
HEADS = (1, 2, 3, 0)
GLOBAL = HG - 1
WINDOW = 32
BLK = 32
NBLK = S // BLK
CH = 512
NCH = S // CH
TPC = CH // P
NT = S // P
BPC = CH // BLK
LOC = CH // (2 * BLK)
E, TOPK, NGRP, TOPG = 16, 4, 4, 2
I = 64
EP = E // 2
NUP = EP + 1
ROUTE_SCALE = 2.5
LN_EPS = 1e-5
Q_SCALE = float(HD) ** -0.5
QTR = 256

ATT, EXP = (0, 1, 2), (3, 4, 5)
ACC, Y = 6, 7
BANKS = 8
LAG_PV = 4
LAG_DOWN = 3
NPROB = 6
NHID = 4
NWT = 3
PAUSE = 2500
ROUTE_PARTS = 7

C32 = {"ident": 128, "vmask": HG * BLK, "eye32": BLK, "onerow": 1, "lower": NGRP * NGRP}
CR = {"pairsel": EP * P, "repeat": 4 * P}
C16 = {"q_a": HG * P, "q_b": HG * P, "k_a": HG * P, "k_b": HG * P, "negmax": P}
CBF = {"identb": 128, "win": CH, "win0": CH}


def fields(sizes):
    at, out = 0, {}
    for name, n in sizes.items():
        out[name] = (at, at + n)
        at += n
    return out, at


def global_tiles():
    return [(j, c, max(BLK * j, CH * c), CH * (c + 1) - max(BLK * j, CH * c))
            for c in range(NCH) for j in range(BPC * (c + 1))]


def global_max_tiles():
    return [(j, c, min(CH, BLK * (j + 1) - CH * c)) for j in range(NBLK) for c in range(j // BPC + 1)]


GT, GM = global_tiles(), global_max_tiles()
CUT = BPC
SCORES = [NBLK // LOC] * (HG - 1) + [len(GT)]
SCORES_BEFORE = [sum(SCORES[:g]) for g in range(HG + 1)]
MAXES = [NBLK // LOC] * (HG - 1) + [len(GM)]


def cost(s):
    kind = s[0]
    if kind in ("score", "max", "pv") and s[1] == GLOBAL:
        cols = (GM if kind == "max" else GT)[s[2]][-1]
        return 60 + cols * (0.45 if kind == "score" else 0.9)
    return {"up": 1600, "down": 860, "q": 640, "k": 640, "v": 500, "vn": 860, "qsel": 430, "ksel": 430, "qfull": 640,
            "score": 500, "max": 600, "pv": 600, "proj": 860, "outT": 430, "xT": 430, "gate": 860, "cwT": 430,
            "route": 1600, "stats": 2500, "ln": 1500, "pads": 1300, "kpads": 1300, "ctx": 2600, "norm": 2000,
            "pause": s[-1]}.get(kind, 0)


def merged(a, b):
    at_a, at_b = sum(map(cost, a)) or 1, sum(map(cost, b)) or 1
    out, i, done_a, done_b = [], 0, 0, 0
    for step in a:
        while i < len(b) and (done_b + cost(b[i]) / 2) / at_b <= done_a / at_a:
            done_b += cost(b[i])
            out.append(b[i])
            i += 1
        out.append(step)
        done_a += cost(step)
    return out + b[i:]


def weight_steps():
    return [("weights", kind, lo, min(lo + 4, NUP)) for kind in range(3) for lo in range(0, NUP, 4)]


def prepare_steps():
    return ([("xT", 0), ("xT", 1), ("gate",)]
            + merged([("pause", 1500), ("q", 0), ("k", 0), ("q", 1), ("k", 1), ("pause", 1500)] + heads_ready(0) + [("pause", 1500)],
                     [("route", i) for i in range(ROUTE_PARTS)]))


def value_steps():
    return [step for c in range(NCH) for step in [("vn", c)] + [("v", c, i) for i in range(4)]]


def heads_ready(g):
    maxes = [("max", g, n) for n in range(MAXES[g])]
    half = CUT if g == GLOBAL else MAXES[g] // 2
    return ([("qsel", g, c) for c in range(NCH)] + [("ksel", g, c) for c in range(NCH)] + [("pads", g)]
            + maxes[:half] + [("maxdone", g, 0), ("kpads", g)] + maxes[half:] + [("maxdone", g, 1)])


def operands(g):
    return [("qfull", g, c) for c in range(NCH)]


def run_steps(g, first=0, last=None):
    out, last = [], SCORES[g] if last is None else last
    for n in range(first, last + LAG_PV):
        if n < last:
            out.append(("score", g, n))
        if n >= first + LAG_PV:
            out.append(("pv", g, n - LAG_PV))
    return out


def expert_steps(c):
    out = []
    for t in range(NUP + LAG_DOWN):
        if 1 <= t <= NUP:
            out.append(("times", c, t - 1))
        if t < NUP:
            out.append(("up", c, t))
        if t >= LAG_DOWN:
            out.append(("down", c, t - LAG_DOWN))
    return out


def gate_steps(c):
    return [("z", c), ("pause", 1000), ("z2", c)]


def output_steps():
    return [("ctx", 1), ("proj", 0), ("mul", 0), ("proj", 1), ("mul", 1), ("outT", 0), ("outT", 1)]


def batch_steps(more):
    local = operands(0) + ([("stats",)] if more else [])
    for g in range(GLOBAL - 1):
        if more and g == 1:
            local += [("ln", 0), ("ln", 1)]
        local += merged(run_steps(g), heads_ready(g + 1) + [("pause", PAUSE)] + operands(g + 1)) + [("norm", g, 0)]
    ready = heads_ready(GLOBAL)
    cut = ready.index(("kpads", GLOBAL)) + 1
    local += merged(run_steps(GLOBAL - 1), ready[:cut] + [("pause", PAUSE), ("qfull", GLOBAL, 0)]) + [("norm", GLOBAL - 1, 0)]
    local += merged(run_steps(GLOBAL, 0, CUT), ready[cut:] + [("pause", PAUSE), ("qfull", GLOBAL, 1)])
    rest = [("norm", GLOBAL, 0), ("ctx", 0)] + run_steps(GLOBAL, CUT) + [("norm", GLOBAL, 1)]
    before = merged(local, expert_steps(1) + gate_steps(1))
    if more:
        return (before + merged(rest, prepare_steps())
                + [("cwT", c) for c in range(NCH)] + merged(output_steps() + value_steps(), expert_steps(0)) + gate_steps(0))
    return before + rest + output_steps()


class Section:

    def __init__(self, steps):
        self.steps, self.place = steps, {}
        self.fills, self.empties = [0] * BANKS, [0] * BANKS
        turns = {ATT: 0, EXP: 0}
        for s in steps:
            if s[0] == "down" and s[2] == 0:
                self.add(("y", s[1]), Y, 0)
            if s[0] == "pv" and s[2] == 0:
                self.add(("acc", s[1], 0), ACC, 0)
            if s == ("pv", GLOBAL, CUT):
                self.add(("acc", GLOBAL, 1), Y, 0)
            if s[0] in ("pv", "down", "norm", "z", "z2", "ln", "stats", "pads", "kpads", "maxdone", "ctx", "route", "times",
                        "mul", "setup", "pause"):
                continue
            ahead = s[0] in ("qsel", "ksel", "max") and s[1] == 0
            ring = EXP if s[0] in ("up", "weights", "xT", "q", "k", "gate") or ahead else ATT
            parts = [s] if s[0] != "up" else [s + (x,) for x in ("gate", "weight", "up") if x != "weight" or s[2] < EP]
            for part in parts:
                self.add(part, ring[turns[ring] % len(ring)], 1)
                turns[ring] += 1

    def add(self, tile, bank, signalled):
        self.place[tile] = (bank, self.fills[bank], self.empties[bank])
        self.fills[bank] += signalled
        self.empties[bank] += 1


FIRST = Section([("stats",), ("ln", 0), ("ln", 1), ("setup",), ("small",)] + merged(prepare_steps(), weight_steps())
                + [("cwT", c) for c in range(NCH)] + merged(value_steps(), expert_steps(0)) + gate_steps(0))
BODY = Section(batch_steps(True))
LAST = Section(batch_steps(False))


class At:

    def __init__(self, section, b):
        self.section, self.b, self.steps = section, b, section.steps
        self.next = 0 if section is FIRST else b + 1

    def bank(self, tile):
        return self.section.place[tile][0]

    def filled(self, tile):
        bank, fills, _ = self.section.place[tile]
        if self.section is FIRST:
            return fills + 1
        return self.b * BODY.fills[bank] + (FIRST.fills[bank] + fills + 1)

    def free(self, tile):
        bank, _, empties = self.section.place[tile]
        if self.section is FIRST:
            return empties + 1
        return self.b * BODY.empties[bank] + (FIRST.empties[bank] + empties + 1)

    def taken(self, tile):
        return self.free(tile) + 1


def build(nc, x, w_qkv, b_qkv, w_out, b_out, gate_w, gate_bias, Wg, Wu, Wd, Ws_g, Ws_u, Ws_d,
          c32, cr, c16, out):
    with ExitStack() as ctx:
        def sb(name, shape, dt=F32):
            return ctx.enter_context(nc.sbuf_tensor(name, shape, dt))

        def sem(name):
            return ctx.enter_context(nc.semaphore(name))

        banks = [ctx.enter_context(nc.psum_tensor(f"bank{i}", [P, CH], F32)) for i in range(BANKS)]

        f32at, n32 = fields(C32)
        f16at, n16 = fields(C16)
        bfat, nbf = fields(CBF)
        frat, nfr = fields(CR)
        k32, k16, kbf = sb("k32", [P, n32]), sb("k16", [P, n16], F16), sb("kbf", [P, nbf], BF16)

        def const32(name):
            return k32[:, f32at[name][0]:f32at[name][1]]

        def const16(name, g=0):
            return k16[:, f16at[name][0] + g * P:f16at[name][0] + (g + 1) * P]

        def constbf(name):
            return kbf[:, bfat[name][0]:bfat[name][1]]

        ident = const32("ident")
        vmask = const32("vmask").rearrange("p (g c) -> p g c", g=HG)
        stage = sb("stage", [P, 3, NUP, P])
        up_hi = sb("up_hi", [P, 2, NUP, P], F32R)
        up_lo = sb("up_lo", [P, 2, NUP, P], F32R)
        down_w = sb("down_w", [P, NUP, P])
        wqkv = sb("wqkv", [P, 3 * D])
        wqk_hi = sb("wqk_hi", [P, 2 * D], F32R)
        wqk_lo = sb("wqk_lo", [P, 2 * D], F32R)
        wout = sb("wout", [P, D])
        gate_nat = sb("gate_nat", [E, D])
        gateT = sb("gateT", [P, E])
        bias3 = sb("bias3", [P, 3])
        bq = sb("bq", [P, 1])
        bo = sb("bo", [P, 1])
        bs = sb("bs", [P, 1])
        gb_row = sb("gb_row", [1, E])
        ones_row = sb("ones_row", [1, P])
        gb = sb("gb", [P, E])
        pairsel = sb("pairsel", [96, EP, P], F32R)
        repeat = sb("repeat", [P, 4, P], F32R)
        vn_hi = sb("vn_hi", [P, CH], F32R)
        vn_lo = sb("vn_lo", [P, CH], F32R)
        half = sb("half", [P, NT])
        xin = sb("xin", [P, NT, D])
        xres = sb("xres", [P, NT, D])
        st6 = sb("st6", [P, NT, 6])
        mv = sb("mv", [P, NT, 2])
        ve = sb("ve", [P, NT])
        y0 = sb("y0", [P, NT])
        nw = sb("nw", [P, NT])
        rstd = sb("rstd", [P, NT])
        xT = sb("xT", [P, S])
        xh = sb("xh", [P, S], F32R)
        xl = sb("xl", [P, S], F32R)
        qkh = sb("qkh", [P, 2, S], F16)
        qkl = sb("qkl", [P, 2, S], F16)
        vbd = sb("vbd", [P, NBLK, HG, 2 * BLK])
        nblk_r = -(-(nfr + nbf) // (HG * 2 * BLK))
        kr = vbd[:, 0:nblk_r].rearrange("p j g c -> p (j g c)")[:, 0:nfr + nbf]
        qtmp = sb("qtmp", [P, S], F16)
        qpad = sb("qpad", [P, NBLK, 4, BLK], F16)
        qall = sb("qall", [P, 2, S], F16)
        kall = sb("kall", [P, 2, S], F16)
        kpad = sb("kpad", [P, 2, NBLK, 4, BLK], F16)
        mxp = sb("mxp", [P, 2, NBLK])
        maxd = sb("maxd", [P, NBLK, BLK], F16)
        prob = stage[:].rearrange("p k t m -> p (k t m)")[:, 0:NPROB * CH].rearrange("p (n q) -> p n q", n=NPROB)
        ctxT = sb("ctxT", [P, S])
        denT = sb("denT", [P, S])
        sT = sb("sT", [P, S])
        qkf = sT[:].rearrange("p (w q) -> p w q", w=2)
        z = sb("z", [P, S])
        th = sb("th", [P, NT, E])
        sc = sb("sc", [P, NT, E])
        sfc = sb("sfc", [P, NT, E])
        pm = sb("pm", [P, 4, NT, NGRP, 2])
        g2 = sb("g2", [P, 2, NT, NGRP])
        gs = sb("gs", [P, NT, NGRP])
        cmp_ = sb("cmp", [P, 2, NT, NGRP, NGRP])
        cnt = sb("cnt", [P, NT, NGRP])
        gm = sb("gm", [P, 2, NT, NGRP])
        msk = sb("msk", [P, NT, E])
        top = sb("top", [P, NT, 8])
        gt = sb("gt", [P, NT, E])
        eq = sb("eq", [P, NT, E])
        pre = sb("pre", [P, 2, NT, 2 * E])
        need = sb("need", [P, NT])
        cw = sb("cw", [P, NT, E])
        wsum = sb("wsum", [P, NT])
        cwT = sb("cwT", [96, S], F32R)
        k96 = ctxT[0:96]
        hid = sb("hid", [P, NHID, CH])
        wrow = sb("wrow", [P, NWT, CH])
        tz = sb("tz", [P, CH])

        filled = [sem(f"bank{i}_filled") for i in range(BANKS)]
        emptied = [sem(f"bank{i}_emptied") for i in range(BANKS)]
        consts_loaded = sem("consts_loaded")
        small_loaded = sem("small_loaded")
        weights_loaded = sem("weights_loaded")
        fills_ready = sem("fills_ready")
        rec_ready = sem("rec_ready")
        small_ready = sem("small_ready")
        x_loaded = sem("x_loaded")
        xres_loaded = sem("xres_loaded")
        var_ready = sem("var_ready")
        pow_ready = sem("pow_ready")
        xn_ready = sem("xn_ready")
        xh_ready = sem("xh_ready")
        xl_ready = sem("xl_ready")
        lo_ready = sem("lo_ready")
        cw_ready = sem("cw_ready")
        qpad_ready = sem("qpad_ready")
        kpad_ready = sem("kpad_ready")
        max_ready = sem("max_ready")
        maxd_ready = sem("maxd_ready")
        pv_done = sem("pv_done")
        down_done = sem("down_done")
        tz_ready = sem("tz_ready")
        z2_ready = sem("z2_ready")
        ctx_ready = sem("ctx_ready")
        hid_ready = sem("hid_ready")
        tanh_ready = sem("tanh_ready")
        o_ready = sem("o_ready")
        stored = [sem(f"stored{c}") for c in range(NCH)]

        x_v = x.rearrange("b (t p) d -> b p t d", p=P)
        out_v = out.rearrange("b (t p) d -> b p t d", p=P)

        def chunk(c):
            return slice(CH * c, CH * (c + 1))

        def sections(eng, walk):
            walk(At(FIRST, 0))
            with eng.Fori(0, B - 1) as b:
                walk(At(BODY, b))
            walk(At(LAST, B - 1))

        def all_taken(eng, at, tiles, own=None):
            last = {at.bank(tile): tile for tile in tiles}
            for bank, tile in last.items():
                if bank != own:
                    eng.wait_ge(emptied[bank], at.taken(tile))

        block = ctx.enter_context(nc.Block())

        @block.sync
        def _(sp):
            sp.dma_start(xin[:], x_v[0]).then_inc(x_loaded, 16)
            sp.dma_start(k32[:], c32).then_inc(consts_loaded, 16)
            sp.dma_start(wqkv[:], w_qkv).then_inc(small_loaded, 16)
            for k in range(3):
                sp.dma_start(bias3[:, k:k + 1], b_qkv[D * k:D * (k + 1)].rearrange("(p a) -> p a", a=1))\
                    .then_inc(small_loaded, 16)
            sp.dma_start(wout[:], w_out).then_inc(small_loaded, 16)
            sp.dma_start(gate_nat[:], gate_w).then_inc(small_loaded, 16)
            sp.dma_start(bo[:], b_out.rearrange("(p a) -> p a", a=1)).then_inc(small_loaded, 16)
            sp.dma_start(gb_row[:], gate_bias.rearrange("(a e) -> a e", a=1)).then_inc(small_loaded, 16)
            sp.dma_start(kr, cr).then_inc(consts_loaded, 16)
            sp.dma_start(k16[:], c16).then_inc(consts_loaded, 16)
            for k, (w, ws) in enumerate(((Wg, Ws_g), (Wu, Ws_u))):
                sp.dma_start(stage[:, k, 0:EP, :], w.rearrange("(t e) i h -> (e i) t h", e=2)).then_inc(weights_loaded, 16)
                sp.dma_start(stage[:, k, EP, :], ws).then_inc(weights_loaded, 16)
            sp.dma_start(stage[:, 2, 0:EP, :].rearrange("h t (e i) -> h (t e) i", e=2),
                         Wd.rearrange("e h i -> h e i")).then_inc(weights_loaded, 16)
            sp.dma_start(stage[:, 2, EP, :], Ws_d).then_inc(weights_loaded, 16)

            def of_batch(v, b):
                return v[b] if isinstance(b, int) else v[bass.ds(b, 1)].rearrange("a p t d -> p (a t) d")

            def batch(at):
                b = at.b
                if at.section is BODY:
                    sp.wait_ge(xl_ready, NCH * b + NCH)
                    sp.dma_start(xin[:], of_batch(x_v, b + 1)).then_inc(x_loaded, 16)
                for c in range(NCH):
                    sp.wait_ge(stored[c], 16 * b + 16)
                sp.dma_start(xres[:], of_batch(x_v, b)).then_inc(xres_loaded, 16)
                for c in range(NCH):
                    sp.wait_ge(emptied[at.bank(("outT", c))], at.taken(("outT", c)))
                    sp.dma_start(of_batch(out_v, b)[:, TPC * c:TPC * (c + 1), :], xres[:, TPC * c:TPC * (c + 1), :])\
                        .then_inc(stored[c], 16)

            with sp.Fori(0, B - 1) as b:
                batch(At(BODY, b))
            batch(At(LAST, B - 1))
            for c in range(NCH):
                sp.wait_ge(stored[c], 16 * (B + 1))

        @block.tensor
        def _(pe):
            def fill(at, tile):
                pe.wait_ge(emptied[at.bank(tile)], at.free(tile))
                return banks[at.bank(tile)]

            def done(at, tile, ins):
                ins.then_inc(filled[at.bank(tile)], 1)

            def parts3(ps, w_hi, w_lo, x_hi, x_lo):
                pe.matmul(ps[:], w_hi, x_hi, start=True, stop=False)
                pe.matmul(ps[:], w_lo, x_hi, start=False, stop=False)
                return pe.matmul(ps[:], w_hi, x_lo, start=False, stop=True)

            def walk(at):
                b, opened = at.b, set()
                for s in at.steps:
                    kind = s[0]
                    if kind == "weights":
                        if s[1] == 0 and s[2] == 0:
                            pe.wait_ge(weights_loaded, 6 * 16)
                        ps = fill(at, s)
                        for i in range(s[2], s[3]):
                            ins = pe.transpose(ps[:, P * (i - s[2]):P * (i - s[2] + 1)], stage[:, s[1], i, :], ident)
                        done(at, s, ins)
                    elif kind == "small":
                        pe.wait_ge(consts_loaded, 48)
                        pe.wait_ge(small_loaded, 8 * 16)
                        pe.wait_ge(small_ready, 1)
                        ps = fill(at, s)
                        pe.transpose(ps[:, 0:E], gate_nat[:], ident[0:E, 0:E])
                        pe.matmul(ps[:, 32:32 + E], ones_row[:], gb_row[:], start=True, stop=True)
                        done(at, s, pe.matmul(ps[:, 64:65], wout[:], bias3[:, 2:3], start=True, stop=True))
                    elif kind == "xT":
                        c = s[1]
                        pe.wait_ge(xn_ready, at.next * NCH + (c + 1))
                        ps = fill(at, s)
                        for i in range(TPC):
                            ins = pe.transpose(ps[:, P * i:P * (i + 1)], xin[:, TPC * c + i, :], ident)
                        done(at, s, ins)
                    elif kind in ("q", "k"):
                        c, w = s[1], "qk".index(kind)
                        if kind == "q":
                            pe.wait_ge(xl_ready, at.next * NCH + (c + 1))
                            if at.section is FIRST and c == 0:
                                pe.wait_ge(small_ready, 2)
                        ps = fill(at, s)
                        done(at, s, parts3(ps, wqk_hi[:, D * w:D * (w + 1)], wqk_lo[:, D * w:D * (w + 1)],
                                           xh[:, chunk(c)], xl[:, chunk(c)]))
                    elif kind == "vn":
                        c = s[1]
                        pe.wait_ge(emptied[at.bank(("xT", c))], at.taken(("xT", c)))
                        ps = fill(at, s)
                        for i in range(TPC):
                            ins = pe.matmul(ps[:, D * i:D * (i + 1)], xT[:, CH * c + P * i:CH * c + P * (i + 1)],
                                            wqkv[:, 2 * D:3 * D], start=True, stop=True)
                        done(at, s, ins)
                    elif kind == "v":
                        c, i = s[1], s[2]
                        if i == 0:
                            pe.wait_ge(emptied[at.bank(("vn", c))], at.taken(("vn", c)))
                        ps = fill(at, s)
                        pe.matmul(ps[:], repeat[:, i, :], vn_hi[:], start=True, stop=False)
                        done(at, s, pe.matmul(ps[:], repeat[:, i, :], vn_lo[:], start=False, stop=True))
                    elif kind == "gate":
                        tiles = [("xT", i) for i in range(NCH)] + ([("small",)] if at.section is FIRST else [])
                        all_taken(pe, at, tiles, at.bank(s))
                        ps = fill(at, s)
                        for t in range(NT):
                            ins = pe.matmul(ps[:, E * t:E * (t + 1)], xT[:, P * t:P * (t + 1)], gateT[:],
                                            start=True, stop=True)
                        done(at, s, ins)
                    elif kind == "cwT":
                        c = s[1]
                        pe.wait_ge(cw_ready, at.next + 1)
                        ps = fill(at, s)
                        for i in range(TPC):
                            ins = pe.transpose(ps[0:E, P * i:P * (i + 1)], cw[:, TPC * c + i, :], ident)
                        done(at, s, ins)
                    elif kind in ("qsel", "ksel", "qfull"):
                        g, c = s[1], s[2]
                        of = b if g else at.next
                        w = 1 if kind == "ksel" else 0
                        if g == 0 and c == 0 and kind == "qsel":
                            pe.wait_ge(lo_ready, of * 2 * NCH + 2 * NCH)
                        if kind == "qfull":
                            pe.wait_ge(maxd_ready, b * HG * NCH + (g * NCH + c + 1))
                        ps = fill(at, s)
                        n = "qk"[w]
                        pe.matmul(ps[:], const16(n + "_a", g), qkh[:, w, chunk(c)], start=True, stop=False)
                        ins = pe.matmul(ps[:], const16(n + "_b", g), qkl[:, w, chunk(c)], start=False,
                                        stop=(kind != "qfull"))
                        if kind == "qfull":
                            ins = pe.matmul(ps[:], const16("negmax"), maxd[:, BPC * c:BPC * (c + 1), :],
                                            start=False, stop=True)
                        done(at, s, ins)
                    elif kind == "max":
                        g, n = s[1], s[2]
                        of = b if g else at.next
                        if n == 0:
                            pe.wait_ge(qpad_ready, of * HG + (g + 1))
                            all_taken(pe, at, [("ksel", g, i) for i in range(NCH)], at.bank(s))
                        ps = fill(at, s)
                        if g == GLOBAL:
                            j, c, cols = GM[n]
                            last = CH * c + cols == BLK * (j + 1)
                            ins = pe.matmul(ps[:, 0:cols], qpad[:, j, :, :], kall[:, g % 2, CH * c:CH * c + cols],
                                            start=True, stop=not last, skip_group_check=True)
                            if last:
                                ins = pe.matmul(ps[:, cols - BLK:cols], constbf("identb"), constbf("win")[:, BLK:2 * BLK],
                                                start=False, stop=True, skip_group_check=True)
                        else:
                            pe.matmul(ps[:], constbf("identb"), constbf("win0" if n == 0 else "win"), start=True, stop=False,
                                      skip_group_check=True)
                            for i in range(LOC):
                                j = LOC * n + i
                                lo = max(0, BLK * (j - 1))
                                cols = BLK * (j + 1) - lo
                                ins = pe.matmul(ps[:, 2 * BLK * (i + 1) - cols:2 * BLK * (i + 1)], qpad[:, j, :, :],
                                                kall[:, g % 2, lo:lo + cols], start=False, stop=(i == LOC - 1),
                                                skip_group_check=True)
                        done(at, s, ins)
                    elif kind == "score":
                        g, n = s[1], s[2]
                        if n == 0 and g != GLOBAL:
                            all_taken(pe, at, [("qfull", g, i) for i in range(NCH)], at.bank(s))
                        elif g == GLOBAL and n in (0, CUT):
                            all_taken(pe, at, [("qfull", g, int(n == CUT))], at.bank(s))
                        if n == 0:
                            pe.wait_ge(kpad_ready, b * HG + (g + 1))
                        ps = fill(at, s)
                        if g == GLOBAL:
                            j, c, q0, cols = GT[n]
                            diag = q0 == BLK * j
                            ins = pe.matmul(ps[:, 0:cols], kpad[:, g % 2, j, :, :], qall[:, g % 2, q0:q0 + cols],
                                            start=True, stop=not diag, skip_group_check=True)
                            if diag:
                                ins = pe.matmul(ps[:, 0:BLK], constbf("identb"), constbf("win")[:, 0:BLK],
                                                start=False, stop=True, skip_group_check=True)
                        else:
                            pe.matmul(ps[:], constbf("identb"), constbf("win"), start=True, stop=False,
                                      skip_group_check=True)
                            for i in range(LOC):
                                j = LOC * n + i
                                cols = min(2 * BLK, S - BLK * j)
                                ins = pe.matmul(ps[:, 2 * BLK * i:2 * BLK * i + cols], kpad[:, g % 2, j, :, :],
                                                qall[:, g % 2, BLK * j:BLK * j + cols], start=False, stop=(i == LOC - 1),
                                                skip_group_check=True)
                        done(at, s, ins)
                    elif kind == "pv":
                        g, n = s[1], s[2]
                        t = SCORES_BEFORE[g] + n
                        half = int(g == GLOBAL and n >= CUT)
                        sums = ("acc", g, half)
                        if n == CUT * half:
                            fill(at, sums)
                            opened = set()
                        acc = banks[at.bank(sums)]
                        tile = ("score", g, n)
                        pe.wait_ge(emptied[at.bank(tile)], at.taken(tile))
                        pieces = []
                        if g == GLOBAL:
                            j, c, q0, cols = GT[n]
                            spans = [(j, q0, 0, cols)]
                        else:
                            spans = [(j, BLK * j, 2 * BLK * (j - LOC * n), min(2 * BLK, S - BLK * j))
                                     for j in range(LOC * n, LOC * (n + 1))]
                        for j, q0, col, cols in spans:
                            q = q0
                            while q < q0 + cols:
                                to = min(q0 + cols, (q // QTR + 1) * QTR)
                                pieces.append((j, q // QTR, q, col + q - q0, to - q))
                                q = to
                        for j, qt, q, col, cols in pieces:
                            r, o = 64 * (qt % 2), QTR * (qt // 2 - half) + q % QTR
                            ins = pe.matmul(acc[r:r + 64, o:o + cols], vbd[:, j, HEADS[g], :], prob[:, t % NPROB, col:col + cols],
                                            start=r not in opened, stop=False, skip_group_check=True)
                            opened.add(r)
                        ins.then_inc(pv_done, 1)
                    elif kind == "proj":
                        c = s[1]
                        pe.wait_ge(ctx_ready, b * NCH + (c + 1))
                        ps = fill(at, s)
                        done(at, s, pe.matmul(ps[:], wout[:], ctxT[:, chunk(c)], start=True, stop=True))
                    elif kind == "up":
                        c, t = s[1], s[2]
                        x_hi, x_lo = xh[:, chunk(c)], xl[:, chunk(c)]
                        gate, up, weight = (s + (x,) for x in ("gate", "up", "weight"))
                        ps = fill(at, gate)
                        done(at, gate, parts3(ps, up_hi[:, 0, t, :], up_lo[:, 0, t, :], x_hi, x_lo))
                        if t < EP:
                            if c == 0 and t == 0:
                                all_taken(pe, at, [("cwT", i) for i in range(NCH)])
                            ps = fill(at, weight)
                            done(at, weight, pe.matmul(ps[:], pairsel[:, t, :], cwT[:, chunk(c)], start=True, stop=True))
                        ps = fill(at, up)
                        done(at, up, parts3(ps, up_hi[:, 1, t, :], up_lo[:, 1, t, :], x_hi, x_lo))
                    elif kind == "down":
                        c, t = s[1], s[2]
                        of = b if c else at.next
                        i = NUP * c + t
                        if t == 0:
                            fill(at, ("y", c))
                        if t < EP:
                            pe.wait_ge(hid_ready, of * NCH * EP + (EP * c + t + 1))
                        else:
                            up = ("up", c, t, "up")
                            pe.wait_ge(emptied[at.bank(up)], at.taken(up))
                        pe.matmul(banks[at.bank(("y", c))][:], down_w[:, t, :], hid[:, i % NHID, :],
                                  start=(t == 0), stop=(t == NUP - 1)).then_inc(down_done, 1)
                    elif kind == "outT":
                        c = s[1]
                        pe.wait_ge(o_ready, b * NCH + (c + 1))
                        ps = fill(at, s)
                        for i in range(TPC):
                            ins = pe.transpose(ps[:, P * i:P * (i + 1)], sT[:, CH * c + P * i:CH * c + P * (i + 1)], ident)
                        done(at, s, ins)

            sections(pe, walk)

        @block.scalar
        def _(act):
            def walk(at):
                b = at.b
                for s in at.steps:
                    kind = s[0]
                    if kind == "up":
                        c, t = s[1], s[2]
                        i = NUP * c + t
                        of = b if c else at.next
                        gate, weight = s + ("gate",), s + ("weight",)
                        act.wait_ge(filled[at.bank(gate)], at.filled(gate))
                        if i >= NHID:
                            act.wait_ge(down_done, of * NCH * NUP + (i - NHID + 1))
                        act.activation(hid[:, i % NHID, :], banks[at.bank(gate)][:], ACT.Tanh, scale=0.5).then_inc(tanh_ready, 1)
                        if t < EP:
                            iw = EP * c + t
                            act.wait_ge(filled[at.bank(weight)], at.filled(weight))
                            if iw >= NWT:
                                act.wait_ge(hid_ready, of * NCH * EP + (iw - NWT + 1))
                            act.activation(wrow[:, iw % NWT, :], banks[at.bank(weight)][:], ACT.Copy)\
                                .then_inc(emptied[at.bank(weight)], 1)
                        continue
                    if kind == "z":
                        c = s[1]
                        act.wait_ge(emptied[Y], at.taken(("y", c)))
                        act.activation(tz[:], z[:, chunk(c)], ACT.Tanh, scale=0.5).then_inc(tz_ready, 1)
                        continue
                    if kind == "norm":
                        g, c = s[1], s[2]
                        done = SCORES_BEFORE[g] + CUT if g == GLOBAL and c == 0 else SCORES_BEFORE[g + 1]
                        act.wait_ge(pv_done, b * SCORES_BEFORE[HG] + done)
                        acc, heads = banks[at.bank(("acc", g, c))], slice(32 * HEADS[g], 32 * HEADS[g] + 32)
                        for u in range(2):
                            for part, to in enumerate((ctxT, denT)):
                                r = 64 * u + 32 * part
                                if g == GLOBAL:
                                    q = CH * c + QTR * u
                                    ins = act.activation(to[heads, q:q + QTR], acc[r:r + 32, 0:QTR], ACT.Copy)
                                else:
                                    ins = act.activation(to[heads, :].rearrange("p (v u q) -> p u v q", u=2, q=QTR)[:, u],
                                                         acc[r:r + 32, :].rearrange("p (v q) -> p v q", q=QTR), ACT.Copy)
                        ins.then_inc(emptied[at.bank(("acc", g, c))], 1)
                        continue
                    if kind not in ("xT", "q", "k", "gate", "qsel", "ksel", "qfull", "score", "proj"):
                        continue
                    ps, freed = banks[at.bank(s)], emptied[at.bank(s)]
                    act.wait_ge(filled[at.bank(s)], at.filled(s))
                    if kind == "q" and at.section is FIRST and s[1] == 0:
                        act.wait_ge(small_ready, 3)
                    if kind == "xT":
                        act.activation(xT[:, chunk(s[1])], ps[:], ACT.Copy).then_inc(freed, 1)
                    elif kind in ("q", "k"):
                        w, c = "qk".index(kind), s[1]
                        scale, bias = (Q_SCALE, bq[:]) if kind == "q" else (1.0, bias3[:, 1:2])
                        if c:
                            act.wait_ge(lo_ready, at.next * 2 * NCH + (2 * c + w - 1))
                        act.activation(qkf[:, w, :], ps[:], ACT.Identity, bias=bias, scale=scale)
                        act.activation(qkh[:, w, chunk(c)], ps[:], ACT.Identity, bias=bias, scale=scale).then_inc(freed, 1)
                    elif kind == "gate":
                        act.activation(th[:].rearrange("p t e -> p (t e)"), ps[:, 0:NT * E], ACT.Tanh, scale=0.5)\
                            .then_inc(freed, 1)
                    elif kind == "qsel":
                        act.activation(qtmp[:, chunk(s[2])], ps[:], ACT.Copy).then_inc(freed, 1)
                    elif kind == "ksel":
                        act.activation(kall[:, s[1] % 2, chunk(s[2])], ps[:], ACT.Identity, bias=const32("onerow"))\
                            .then_inc(freed, 1)
                    elif kind == "qfull":
                        act.activation(qall[:, s[1] % 2, chunk(s[2])], ps[:], ACT.Copy).then_inc(freed, 1)
                    elif kind == "score":
                        g, n = s[1], s[2]
                        t = SCORES_BEFORE[g] + n
                        cols = GT[n][3] if g == GLOBAL else CH
                        if t >= NPROB:
                            act.wait_ge(pv_done, b * SCORES_BEFORE[HG] + (t - NPROB + 1))
                        act.activation(prob[:, t % NPROB, 0:cols], ps[:, 0:cols], ACT.Exp).then_inc(freed, 1)
                    elif kind == "proj":
                        act.activation(sT[:, chunk(s[1])], ps[:], ACT.Identity, bias=bs[:], scale=0.5).then_inc(freed, 1)

            sections(act, walk)

        @block.vector
        def _(dve):
            def credits():
                for r in emptied:
                    dve.sem_inc(r, 1)
                for st in stored:
                    dve.sem_inc(st, 16)
                dve.memset(ones_row[:], 1.0).then_inc(small_ready, 1)

            def setup():
                dve.wait_ge(consts_loaded, 48)
                dve.wait_ge(small_loaded, 8 * 16)
                dve.wait_ge(fills_ready, 1)
                dve.tensor_scalar(bq[:], bias3[:, 0:1], Q_SCALE, None, ALU.mult)
                dve.tensor_copy(wqk_hi[:], wqkv[:, 0:2 * D])
                dve.drain()
                dve.tensor_tensor(wqk_lo[:], wqkv[:, 0:2 * D], wqk_hi[:].bitcast(F32), ALU.subtract)\
                    .then_inc(small_ready, 2)
                dve.tensor_copy(cwT[:], k96)
                dve.tensor_scalar(pairsel[:].rearrange("p t m -> p (t m)"), kr[0:96, frat["pairsel"][0]:frat["pairsel"][1]],
                                  0.5, None, ALU.mult)
                dve.tensor_copy(kbf[:], kr[:, nfr:nfr + nbf])
                dve.tensor_copy(repeat[:].rearrange("p i m -> p (i m)"), kr[:, frat["repeat"][0]:frat["repeat"][1]])
                dve.drain()
                dve.tensor_copy(vbd[:, :, :, BLK:2 * BLK].rearrange("p j g c -> p j (g) c"),
                                vmask.unsqueeze(1).broadcast_to([P, NBLK, HG, BLK]))

            def tt(out_, a, b_, op):
                return dve.tensor_tensor(out_, a, b_, op)

            def ts(out_, a, s1, s2, op0, op1=None):
                return dve.tensor_scalar(out_, a, s1, s2, op0, op1) if op1 else dve.tensor_scalar(out_, a, s1, s2, op0)

            def routing(part):
                def over(a, shape, axis):
                    return a.unsqueeze(axis).broadcast_to(shape)

                NG = [P, NT, NGRP, NGRP]
                pairs = sfc[:].rearrange("p t (g a b) -> p (t g) a b", g=NGRP, a=2)
                flat = [pm[:, i].rearrange("p t g a -> p (t g) a") for i in range(4)]
                g2f = [g2[:, i].rearrange("p t g -> p (t g)") for i in range(2)]
                other, own = over(gs[:], NG, 2), over(gs[:], NG, 3)
                lower = const32("lower").rearrange("p (i j) -> p i j", i=NGRP)
                of_group = "p t (g e) -> p t g e"
                kth = top[:, :, TOPK - 1:TOPK].broadcast_to([P, NT, E])
                run = pre[:, 0, :, E:2 * E]
                if part == 0:
                    ts(sc[:], th[:], 0.5, 0.5, ALU.mult, ALU.add)
                    dve.drain()
                    tt(sfc[:], sc[:], over(gb[:], [P, NT, E], 1), ALU.add)
                    dve.drain()
                    tt(flat[0], pairs[:, :, :, 0], pairs[:, :, :, 1], ALU.max)
                    tt(flat[1], pairs[:, :, :, 0], pairs[:, :, :, 1], ALU.min)
                    dve.drain()
                    tt(g2f[0], flat[0][:, :, 0], flat[0][:, :, 1], ALU.max)
                    tt(flat[2][:, :, 0], flat[0][:, :, 0], flat[0][:, :, 1], ALU.min)
                    tt(flat[2][:, :, 1], flat[1][:, :, 0], flat[1][:, :, 1], ALU.max)
                elif part == 1:
                    dve.drain()
                    tt(g2f[1], flat[2][:, :, 0], flat[2][:, :, 1], ALU.max)
                    dve.drain()
                    tt(gs[:], g2[:, 0], g2[:, 1], ALU.add)
                    dve.drain()
                    tt(cmp_[:, 0], other, own, ALU.is_gt)
                    tt(cmp_[:, 1], other, own, ALU.is_ge)
                    dve.drain()
                    tt(cmp_[:, 1], cmp_[:, 1], cmp_[:, 0], ALU.subtract)
                elif part == 2:
                    dve.drain()
                    tt(cmp_[:, 1], cmp_[:, 1], over(lower, NG, 1), ALU.mult)
                    dve.drain()
                    tt(cmp_[:, 0], cmp_[:, 0], cmp_[:, 1], ALU.add)
                    dve.drain()
                    dve.tensor_reduce(cnt[:], cmp_[:, 0], AX_X, ALU.add)
                    dve.drain()
                    ts(gm[:, 0], cnt[:], float(TOPG), None, ALU.is_lt)
                    ts(gm[:, 1], cnt[:], float(TOPG), -1e30, ALU.is_ge, ALU.mult)
                elif part == 3:
                    dve.drain()
                    tt(msk[:].rearrange(of_group, g=NGRP), sfc[:].rearrange(of_group, g=NGRP), over(gm[:, 0], NG, 3), ALU.mult)
                    dve.drain()
                    tt(msk[:].rearrange(of_group, g=NGRP), msk[:].rearrange(of_group, g=NGRP), over(gm[:, 1], NG, 3), ALU.add)
                    dve.drain()
                    for t in range(NT):
                        dve.max(top[:, t, :], msk[:, t, :])
                    dve.drain()
                    tt(gt[:], msk[:], kth, ALU.is_gt)
                    tt(eq[:], msk[:], kth, ALU.is_equal)
                    tt(pre[:, 0, :, E:2 * E], msk[:], kth, ALU.is_equal)
                elif part == 4:
                    dve.drain()
                    dve.tensor_reduce(need[:], gt[:], AX_X, ALU.add)
                    src = 0
                    for sh in (1, 2, 4, 8):
                        tt(pre[:, 1 - src, :, E:2 * E], pre[:, src, :, E:2 * E], pre[:, src, :, E - sh:2 * E - sh], ALU.add)
                        dve.drain()
                        src = 1 - src
                    tt(run, run, over(need[:], [P, NT, E], 2), ALU.add)
                    dve.drain()
                    ts(run, run, float(TOPK), None, ALU.is_le)
                    dve.drain()
                    tt(eq[:], eq[:], run, ALU.mult)
                elif part == 5:
                    dve.drain()
                    tt(gt[:], gt[:], eq[:], ALU.add)
                    dve.drain()
                    tt(msk[:], sc[:], gt[:], ALU.mult)
                    dve.drain()
                    dve.tensor_reduce(need[:], msk[:], AX_X, ALU.add)
                    dve.drain()
                    ts(need[:], need[:], 1e-20, None, ALU.add)
                elif part == 6:
                    dve.drain()
                    dve.reciprocal(wsum[:], need[:])
                    dve.drain()
                    dve.scalar_tensor_tensor(out=cw[:], in0=msk[:], scalar=ROUTE_SCALE, in1=over(wsum[:], [P, NT, E], 2),
                                             op0=ALU.mult, op1=ALU.mult).then_inc(cw_ready, 1)


            def walk(at):
                b = at.b
                if at.section is FIRST:
                    credits()
                for s in at.steps:
                    kind = s[0]
                    if kind == "stats":
                        dve.wait_ge(x_loaded, at.next * 16 + 16)
                        for t in range(NT):
                            dve.bn_stats(st6[:, t, :], xin[:, t, :])
                        dve.drain()
                        for t in range(NT):
                            dve.bn_aggr(mv[:, t, :], st6[:, t, :])
                        dve.drain()
                        ts(ve[:], mv[:, :, 1], LN_EPS, None, ALU.add).then_inc(var_ready, 1)
                    elif kind == "ln":
                        c = s[1]
                        if c == 0:
                            dve.wait_ge(pow_ready, at.next + 1)
                            tt(nw[:], y0[:], y0[:], ALU.mult)
                            dve.drain()
                            tt(nw[:], nw[:], ve[:], ALU.mult)
                            dve.drain()
                            ts(nw[:], nw[:], -0.5, 1.5, ALU.mult, ALU.add)
                            dve.drain()
                            tt(rstd[:], y0[:], nw[:], ALU.mult)
                            dve.drain()
                        for t in range(TPC * c, TPC * (c + 1)):
                            ins = ts(xin[:, t, :], xin[:, t, :], mv[:, t, 0:1], rstd[:, t:t + 1], ALU.subtract, ALU.mult)
                        ins.then_inc(xn_ready, 1)
                    elif kind == "xT":
                        dve.wait_ge(emptied[at.bank(s)], at.taken(s))
                        dve.tensor_copy(xh[:, chunk(s[1])], xT[:, chunk(s[1])]).then_inc(xh_ready, 1)
                    elif kind == "pads":
                        g = s[1]
                        all_taken(dve, at, [("qsel", g, i) for i in range(NCH)])
                        for h in range(4):
                            r = slice(32 * h, 32 * h + 32)
                            ins = dve.tensor_copy(qpad[r, :, h, :], qtmp[r, :].rearrange("p (j q) -> p j q", q=BLK))
                        ins.then_inc(qpad_ready, 1)
                    elif kind in ("maxdone", "kpads"):
                        g = s[1]
                        if kind == "maxdone":
                            if g != GLOBAL or s[2] == 0:
                                continue
                            dve.drain()
                            tt(mxp[:, 0, BPC:NBLK], mxp[:, 0, BPC:NBLK], mxp[:, 1, BPC:NBLK], ALU.max).then_inc(max_ready, 1)
                            continue
                        all_taken(dve, at, [("ksel", g, i) for i in range(NCH)])
                        for h in range(4):
                            r = slice(32 * h, 32 * h + 32)
                            ins = dve.tensor_copy(kpad[r, g % 2, :, h, :], kall[r, g % 2, :].rearrange("p (j q) -> p j q", q=BLK))
                        ins.then_inc(kpad_ready, 1)
                    elif kind == "setup":
                        setup()
                    elif kind == "route":
                        if s[1] == 0:
                            dve.wait_ge(emptied[at.bank(("gate",))], at.taken(("gate",)))
                        routing(s[1])
                    elif kind == "ctx":
                        c = s[1]
                        sums = ("acc", GLOBAL, c)
                        dve.wait_ge(emptied[at.bank(sums)], at.taken(sums))
                        dve.reciprocal(denT[:, chunk(c)], denT[:, chunk(c)]).then_inc(rec_ready, 1)
                    elif kind == "z":
                        c = s[1]
                        of = b if c else at.next
                        dve.wait_ge(down_done, of * NCH * NUP + NUP * (c + 1))
                        tt(z[:, chunk(c)], xT[:, chunk(c)], banks[Y][:], ALU.add).then_inc(emptied[Y], 1)
                    elif kind == "z2":
                        c = s[1]
                        dve.wait_ge(tz_ready, (b if c else at.next) * NCH + (c + 1))
                        dve.scalar_tensor_tensor(out=z[:, chunk(c)], in0=tz[:], scalar=1.0, in1=z[:, chunk(c)],
                                                 op0=ALU.add, op1=ALU.mult).then_inc(z2_ready, 1)
                    elif kind == "up":
                        i = NUP * s[1] + s[2]
                        gate = s + ("gate",)
                        dve.wait_ge(tanh_ready, (b if s[1] else at.next) * NCH * NUP + (i + 1))
                        dve.scalar_tensor_tensor(out=hid[:, i % NHID, :], in0=hid[:, i % NHID, :], scalar=1.0,
                                                 in1=banks[at.bank(gate)][:], op0=ALU.add, op1=ALU.mult)\
                            .then_inc(emptied[at.bank(gate)], 1)
                    elif kind == "times":
                        c, t = s[1], s[2]
                        i = NUP * c + t
                        gate, up = ("up", c, t, "gate"), ("up", c, t, "up")
                        dve.wait_ge(emptied[at.bank(gate)], at.taken(gate))
                        dve.wait_ge(filled[at.bank(up)], at.filled(up))
                        tt(hid[:, i % NHID, :], hid[:, i % NHID, :], banks[at.bank(up)][:], ALU.mult)\
                            .then_inc(emptied[at.bank(up)], 1)
                    elif kind in ("weights", "small", "vn", "v", "cwT", "max", "outT"):
                        ps, freed = banks[at.bank(s)], emptied[at.bank(s)]
                        dve.wait_ge(filled[at.bank(s)], at.filled(s))
                        if kind == "weights":
                            k, lo, hi = s[1], s[2], s[3]
                            tile = ps[:, 0:P * (hi - lo)].rearrange("p (t m) -> p t m", m=P)
                            if k == 2 and hi == NUP:
                                ts(down_w[:, lo:hi, :], tile, 0.5, None, ALU.mult).then_inc(freed, 1)
                            elif k == 2:
                                dve.tensor_copy(down_w[:, lo:hi, :], tile).then_inc(freed, 1)
                            else:
                                dve.tensor_copy(up_hi[:, k, lo:hi, :], tile)
                                dve.drain()
                                tt(up_lo[:, k, lo:hi, :], tile, up_hi[:, k, lo:hi, :].bitcast(F32), ALU.subtract).then_inc(freed, 1)
                        elif kind == "small":
                            dve.tensor_copy(gateT[:], ps[:, 0:E])
                            dve.tensor_copy(gb[:], ps[:, 32:32 + E])
                            ts(bs[:], ps[:, 64:65], bo[:], 0.5, ALU.add, ALU.mult).then_inc(freed, 1)
                        elif kind == "vn":
                            dve.tensor_copy(vn_hi[:], ps[:])
                            dve.drain()
                            tt(vn_lo[:], ps[:], vn_hi[:].bitcast(F32), ALU.subtract).then_inc(freed, 1)
                        elif kind == "v":
                            c, i = s[1], s[2]
                            tt(vbd[:].rearrange("p (t i) g c -> p i t g c", i=4)[:, i, TPC * c:TPC * (c + 1), :, 0:BLK],
                               ps[:].rearrange("p (j g c) -> p j g c", j=4, g=HG),
                               vmask.unsqueeze(1).broadcast_to([P, 4, HG, BLK]), ALU.mult).then_inc(freed, 1)
                        elif kind == "cwT":
                            c = s[1]
                            dve.tensor_copy(cwT[0:E, chunk(c)], ps[0:E, :])
                            dve.drain()
                            tt(cwT[32:32 + E, chunk(c)], ps[0:E, :], cwT[0:E, chunk(c)].bitcast(F32), ALU.subtract).then_inc(freed, 1)
                        elif kind == "max":
                            g, n = s[1], s[2]
                            if g == GLOBAL:
                                j, c, cols = GM[n]
                                ins = dve.tensor_reduce(mxp[:, c, j:j + 1], ps[:, 0:cols], AX_X, ALU.max)
                            else:
                                ins = dve.tensor_reduce(mxp[:, 0, LOC * n:LOC * (n + 1)],
                                                        ps[:].rearrange("p (j q) -> p j q", q=2 * BLK), AX_X, ALU.max)
                            ins.then_inc(freed, 1)
                        elif kind == "outT":
                            c = s[1]
                            dve.wait_ge(xres_loaded, b * 16 + 16)
                            tt(xres[:, TPC * c:TPC * (c + 1), :], xres[:, TPC * c:TPC * (c + 1), :],
                               ps[:].rearrange("p (t d) -> p t d", d=D), ALU.add).then_inc(freed, 1)

            sections(dve, walk)

        @block.gpsimd
        def _(pool):
            def walk(at):
                b = at.b
                if at.section is FIRST:
                    pool.memset(half[:], -0.5)
                    pool.memset(pre[:], 0.0)
                    pool.memset(qpad[:], 0.0)
                    pool.memset(kpad[:], 0.0)
                    pool.memset(k96, 0.0).then_inc(fills_ready, 1)
                    pool.drain()
                for s in at.steps:
                    kind = s[0]
                    if kind == "stats":
                        pool.wait_ge(var_ready, at.next + 1)
                        pool.tensor_tensor(y0[:], ve[:], half[:], ALU.pow).then_inc(pow_ready, 1)
                    elif kind == "xT":
                        c = s[1]
                        pool.wait_ge(xh_ready, at.next * NCH + (c + 1))
                        pool.tensor_tensor(xl[:, chunk(c)], xT[:, chunk(c)], xh[:, chunk(c)].bitcast(F32), ALU.subtract)\
                            .then_inc(xl_ready, 1)
                    elif kind in ("q", "k"):
                        w, c = "qk".index(kind), s[1]
                        pool.wait_ge(emptied[at.bank(s)], at.taken(s))
                        pool.tensor_tensor(qkl[:, w, chunk(c)], qkf[:, w, :], qkh[:, w, chunk(c)], ALU.subtract)\
                            .then_inc(lo_ready, 1)
                    elif kind == "maxdone":
                        g, c = s[1], s[2]
                        if g == GLOBAL and c == 1:
                            pool.wait_ge(max_ready, b + 1)
                        else:
                            tile = ("max", g, CUT - 1 if g == GLOBAL else MAXES[g] // 2 * (c + 1) - 1)
                            pool.wait_ge(emptied[at.bank(tile)], at.taken(tile))
                        blocks = slice(BPC * c, BPC * (c + 1))
                        pool.tensor_tensor(maxd[:, blocks, :], mxp[:, 0, blocks].unsqueeze(2).broadcast_to([P, BPC, BLK]),
                                           const32("eye32").unsqueeze(1).broadcast_to([P, BPC, BLK]), ALU.mult)\
                            .then_inc(maxd_ready, 1)
                    elif kind == "times" and s[2] < EP:
                        c, t = s[1], s[2]
                        up, weight = ("up", c, t, "up"), ("up", c, t, "weight")
                        i, iw = NUP * c + t, EP * c + t
                        pool.wait_ge(emptied[at.bank(weight)], at.taken(weight))
                        pool.wait_ge(emptied[at.bank(up)], at.taken(up))
                        pool.tensor_tensor(hid[:, i % NHID, :], hid[:, i % NHID, :], wrow[:, iw % NWT, :], ALU.mult)\
                            .then_inc(hid_ready, 1)
                    elif kind == "ctx":
                        c = s[1]
                        pool.wait_ge(rec_ready, b * NCH + (c + 1))
                        pool.tensor_tensor(ctxT[:, chunk(c)], ctxT[:, chunk(c)], denT[:, chunk(c)], ALU.mult)\
                            .then_inc(ctx_ready, 1)
                    elif kind == "mul":
                        c = s[1]
                        pool.wait_ge(z2_ready, b * NCH + (c + 1))
                        pool.wait_ge(emptied[at.bank(("proj", c))], at.taken(("proj", c)))
                        pool.tensor_tensor(sT[:, chunk(c)], sT[:, chunk(c)], z[:, chunk(c)], ALU.mult).then_inc(o_ready, 1)

            sections(pool, walk)


_INS = ["L0_attn_x", "L0_attn_w_qkv", "L0_attn_b_qkv", "L0_attn_w_out", "L0_attn_b_out", "L0_ffn_gate_w",
        "L0_ffn_gate_bias", "L0_ffn_Wg", "L0_ffn_Wu", "L0_ffn_Wd", "L0_ffn_Ws_g", "L0_ffn_Ws_u", "L0_ffn_Ws_d"]
_OUTS = [((B, S, D), "float32")]


def constants():
    import numpy as np

    rows, cols = np.arange(P)[:, None], np.arange(P)[None, :]
    head, r = rows // BLK, rows % BLK
    f32 = {
        "ident": rows == cols,
        "vmask": np.tile(head == np.arange(BLK)[None, :] // HD, (1, HG)),
        "eye32": r == np.arange(BLK)[None, :],
        "onerow": r == 3 * HD,
    }
    fr = {
        "pairsel": (rows % BLK == np.arange(EP * P)[None, :] // I) & (rows < 2 * BLK),
        "repeat": rows == BLK * (np.arange(4 * P)[None, :] // P) + np.arange(4 * P)[None, :] % BLK,
    }
    f32 |= {
        "lower": np.tile((np.arange(NGRP)[None, :] < np.arange(NGRP)[:, None]).reshape(1, -1), (P, 1)),
    }
    feature_head, dim = rows // HD, rows % HD

    def select(g, groups):
        out = np.zeros((P, P), bool)
        for part in groups:
            out |= cols == (feature_head - 4 * g) * BLK + part * HD + dim
        return out & (feature_head // 4 == g)

    f16 = {name: np.concatenate([select(g, groups) for g in HEADS], 1)
           for name, groups in (("q_a", (0, 2)), ("q_b", (1,)), ("k_a", (0, 1)), ("k_b", (2,)))}
    f16["negmax"] = -1.0 * (cols == head * BLK + 3 * HD)
    c = np.arange(CH)[None, :]
    inside = (c % (2 * BLK) >= r) & (c % (2 * BLK) <= r + WINDOW)
    bf = {
        "identb": 1.0 * (rows == cols),
        "win": np.where(inside, 0.0, -1e30),
        "win0": np.where(inside & (c >= BLK), 0.0, -1e30),
    }

    def packed(parts, sizes, dtype):
        return np.concatenate([np.asarray(parts[n]).astype(dtype) for n in sizes], 1)

    return {"c32": packed(f32, C32, np.float32), "cr": packed(fr | bf, CR | CBF, np.float32),
            "c16": packed(f16, C16, np.float16)}


def kernel(**inputs):
    import numpy as _np
    import concourse.bacc as _bacc
    from concourse import mybir as _mybir
    from concourse.bass_utils import run_bass_kernel_spmd as _run

    nc = _bacc.Bacc("TRN2", target_bir_lowering=False, num_devices=1)
    arrays, args = {}, []
    for name, a in [(n, _np.ascontiguousarray(inputs[n])) for n in _INS] + list(constants().items()):
        arrays[f"in_{name}_dram"] = a
        args.append(nc.dram_tensor(f"in_{name}_dram", a.shape, _mybir.dt.from_np(a.dtype), kind="ExternalInput").ap())
    for i, (shape, dtype) in enumerate(_OUTS):
        dt = _mybir.dt.from_np(_np.dtype(dtype))
        args.append(nc.dram_tensor(f"out_{i}_dram", shape, dt, kind="ExternalOutput").ap())
    build(nc, *args)
    r = _run(nc, [arrays], core_ids=[0])
    got = tuple(r.results[0][f"out_{i}_dram"] for i in range(len(_OUTS)))
    return got[0]
```

```python
from contextlib import ExitStack

import concourse.bass as bass
from concourse import mybir

F32 = mybir.dt.float32
F32R = mybir.dt.float32r
F16 = mybir.dt.float16
BF16 = mybir.dt.bfloat16
ALU = mybir.AluOpType
ACT = mybir.ActivationFunctionType
AX_X = mybir.AxisListType.X

P = 128
B, S, D = 4, 1024, 128
H, HD = 16, 8
HG = H // 4
HEADS = (1, 2, 3, 0)
GLOBAL = HG - 1
WINDOW = 32
BLK = 32
NBLK = S // BLK
CH = 512
NCH = S // CH
TPC = CH // P
NT = S // P
BPC = CH // BLK
LOC = CH // (2 * BLK)
E, TOPK, NGRP, TOPG = 16, 4, 4, 2
I = 64
EP = E // 2
NUP = EP + 1
ROUTE_SCALE = 2.5
LN_EPS = 1e-5
Q_SCALE = float(HD) ** -0.5
QTR = 256

ATT, EXP = (0, 1, 2), (3, 4, 5)
ACC, Y = 6, 7
BANKS = 8
LAG_PV = 4
LAG_DOWN = 3
NPROB = 6
NHID = 5
NWT = 3
SPLIT_PAIR = 6
MAX_BEFORE = 1
MAX_BEHIND = 2
CTX0 = 26
CTX1 = 38
ROUTE_PARTS = 7

C32 = {"ident": 128, "vmask": HG * BLK, "eye32": BLK, "onerow": 1, "lower": NGRP * NGRP, "win": 2 * BLK, "win0": 2 * BLK}
C16 = {"q_a": HG * P, "q_b": HG * P, "k_a": HG * P, "k_b": HG * P, "negmax": P, "eye": P}
CBF = {"identb": 128, "win": CH, "win0": CH}


def fields(sizes):
    at, out = 0, {}
    for name, n in sizes.items():
        out[name] = (at, at + n)
        at += n
    return out, at


def global_tiles():
    return [(j, c, max(BLK * j, CH * c), CH * (c + 1) - max(BLK * j, CH * c))
            for c in range(NCH) for j in range(BPC * (c + 1))]


def global_max_tiles():
    return [(j, c, min(CH, BLK * (j + 1) - CH * c)) for j in range(NBLK) for c in range(j // BPC + 1)]


GT, GM = global_tiles(), global_max_tiles()
CUT = BPC
SCORES = [NBLK // LOC] * (HG - 1) + [len(GT)]
SCORES_BEFORE = [sum(SCORES[:g]) for g in range(HG + 1)]
MAXES = [NBLK // LOC] * (HG - 1) + [len(GM)]


COST = {"up": 1920, "down": 860, "q": 640, "k": 2688, "v": 350, "vn": 860, "qsel": 516, "ksel": 516,
        "qfull": 600, "score": 500, "max": 510, "pv": 180, "proj": 2580, "outT": 365, "xT": 430, "gate": 2580,
        "cwT": 602, "route": 1120, "stats": 2500, "ln": 1500, "pads": 1560, "kpads": 1105, "ctx": 1300,
        "norm": 2000, "weights": 1200}
COLUMN = {"score": 0.54, "max": 0.9, "pv": 2.7}
PAUSES = {"pads": 10, "maxdone": 2500, "global0": 2500, "global1": 2500, "xT": 450, "q": 1547, "qk": 2600,
          "route": 450, "cwT": 1116, "out": 2, "z": 1750, "experts": 3, "second": 3, "routing": 3, "values": 3,
          "rest": 1275, "ctx": 5, "early": 2486}


def pause(name):
    return ("pause", PAUSES[name])


def cost(s):
    kind = s[0]
    if kind == "pause":
        return s[1]
    if kind in COLUMN and s[1] == GLOBAL:
        return 60 + (GM if kind == "max" else GT)[s[2]][-1] * COLUMN[kind]
    return COST.get(kind, 0)


def merged(a, b):
    at_a, at_b = sum(map(cost, a)) or 1, sum(map(cost, b)) or 1
    out, i, done_a, done_b = [], 0, 0, 0
    for step in a:
        while i < len(b) and (done_b + cost(b[i]) / 2) / at_b <= done_a / at_a:
            done_b += cost(b[i])
            out.append(b[i])
            i += 1
        out.append(step)
        done_a += cost(step)
    return out + b[i:]


WEIGHT_TILES = [("weights", kind, lo, min(lo + 4, NUP)) for kind in range(3) for lo in range(0, NUP, 4)]


def prepare_steps():
    return ([("xT", 0), ("xT", 1), pause("xT"), ("gate",)]
            + merged([pause("q"), ("q", 0), ("k", 0), ("q", 1), ("k", 1), pause("qk")] + heads_ready(0) + [pause("route")],
                     [pause("routing")] + [("route", i) for i in range(ROUTE_PARTS)]))


def value_steps():
    return [step for c in range(NCH) for step in [("vn", c)] + [("v", c, i) for i in range(4)]]


def heads_ready(g):
    maxes = [("max", g, n) for n in range(MAXES[g])]
    half = CUT if g == GLOBAL else MAXES[g] // 2
    return ([("qsel", g, c) for c in range(NCH)] + [("ksel", g, c) for c in range(NCH)] + [("pads", g), pause("pads")]
            + maxes[:half] + [("maxdone", g, 0), ("kpads", g)] + maxes[half:] + [("maxdone", g, 1)])


def operands(g):
    return [("qfull", g, c) for c in range(NCH)]


def run_steps(g, first=0, last=None):
    out, last = [], SCORES[g] if last is None else last
    for n in range(first, last + LAG_PV):
        if n < last:
            out.append(("score", g, n))
        if n >= first + LAG_PV:
            out.append(("pv", g, n - LAG_PV))
    return out


def expert_steps(c):
    out = []
    for t in range(NUP + LAG_DOWN):
        if 1 <= t <= NUP:
            out.append(("times", c, t - 1))
        if t < NUP:
            out.append(("up", c, t))
        if t >= LAG_DOWN:
            out.append(("down", c, t - LAG_DOWN))
    return out


def gate_steps(c):
    return [("z", c), pause("z"), ("z2", c)]


FIRST_EXPERTS = expert_steps(0) + gate_steps(0)
SPLIT = FIRST_EXPERTS.index(("up", 0, SPLIT_PAIR))


def output_steps():
    return [("ctx", 1, 0), pause("ctx"), ("ctx", 1, 1), ("proj", 0), ("mul", 0), ("proj", 1), ("mul", 1), ("outT", 0), ("outT", 1)]


def batch_steps(more):
    local = operands(0) + ([("stats",)] if more else [])
    for g in range(GLOBAL - 1):
        if more and g == 1:
            local += [("ln", 0), ("ln", 1)]
        local += merged(run_steps(g), heads_ready(g + 1) + [pause("maxdone")] + operands(g + 1)) + [("norm", g, 0)]
    ready = heads_ready(GLOBAL)
    cut = ready.index(("kpads", GLOBAL)) + 1
    local += merged(run_steps(GLOBAL - 1), ready[:cut] + [pause("global0")]) + [("norm", GLOBAL - 1, 0)]
    local += ready[cut:cut + MAX_BEFORE] + [("qfull", GLOBAL, 0)] + ready[cut + MAX_BEFORE:cut + MAX_BEFORE + MAX_BEHIND]
    local += merged(run_steps(GLOBAL, 0, CUT), ready[cut + MAX_BEFORE + MAX_BEHIND:] + [pause("global1"), ("qfull", GLOBAL, 1)])
    rest = run_steps(GLOBAL, CUT) + [("norm", GLOBAL, 1)]
    rest[CTX0:CTX0] = [("ctx", 0, 0)]
    rest[CTX1:CTX1] = [("ctx", 0, 1)]
    rest = [("norm", GLOBAL, 0), pause("rest")] + rest
    before = merged(local, FIRST_EXPERTS[SPLIT:] + [pause("second")] + expert_steps(1) + gate_steps(1))
    if more:
        return (before + merged(rest, prepare_steps() + [pause("cwT")] + [("cwT", c) for c in range(NCH)])
                + merged([pause("out")] + output_steps() + [pause("values")] + value_steps(), [pause("experts")] + FIRST_EXPERTS[:SPLIT]))
    out = output_steps()
    early = [("proj", 0), ("mul", 0), ("outT", 0)]
    return before + merged(rest, [pause("early")] + early) + [s for s in out if s not in early]


class Section:

    def __init__(self, steps):
        self.steps, self.place = steps, {}
        self.fills, self.empties = [0] * BANKS, [0] * BANKS
        turns = {ATT: 0, EXP: 0}
        for s in steps:
            if s[0] == "down" and s[2] == 0:
                self.place[("y", s[1])] = (Y, self.fills[Y], self.empties[Y])
            if s[0] == "z":
                self.add(("z", s[1]), Y, 0)
            if s[0] == "pv" and s[2] == 0:
                self.add(("acc", s[1], 0), ACC, 0)
            if s == ("pv", GLOBAL, CUT):
                self.add(("acc", GLOBAL, 1), Y, 0)
            if s[0] in ("pv", "down", "norm", "z", "z2", "ln", "stats", "pads", "kpads", "maxdone", "ctx", "route", "times",
                        "mul", "setup", "fill", "ones", "pause"):
                continue
            ahead = s[0] in ("qsel", "ksel", "max") and s[1] == 0
            ring = EXP if s[0] in ("up", "weights", "xT", "q", "k", "gate") or ahead else ATT
            parts = [s] if s[0] != "up" else [s + (x,) for x in ("weight", "gate", "up") if x != "weight" or s[2] < EP]
            for part in parts:
                self.add(part, ring[turns[ring] % len(ring)], 1)
                turns[ring] += 1

    def add(self, tile, bank, signalled):
        self.place[tile] = (bank, self.fills[bank], self.empties[bank])
        self.fills[bank] += signalled
        self.empties[bank] += 1


FIRST = Section([("stats",), ("fill", 0), ("ln", 0), ("ln", 1), ("setup",), ("small",)]
                + merged(prepare_steps(), [("fill", 1)] + WEIGHT_TILES) + [("vbias",), ("ones",)]
                + [("cwT", c) for c in range(NCH)] + merged(value_steps(), FIRST_EXPERTS[:SPLIT]))
BODY = Section(batch_steps(True))
LAST = Section(batch_steps(False))


class At:

    def __init__(self, section, b):
        self.section, self.b, self.steps = section, b, section.steps
        self.next = 0 if section is FIRST else b + 1

    def of(self, step):
        return self.next if step in FIRST_EXPERTS[:SPLIT] else self.b

    def bank(self, tile):
        return self.section.place[tile][0]

    def filled(self, tile):
        bank, fills, _ = self.section.place[tile]
        if self.section is FIRST:
            return fills + 1
        return self.b * BODY.fills[bank] + (FIRST.fills[bank] + fills + 1)

    def free(self, tile):
        bank, _, empties = self.section.place[tile]
        if self.section is FIRST:
            return empties + 1
        return self.b * BODY.empties[bank] + (FIRST.empties[bank] + empties + 1)

    def taken(self, tile):
        return self.free(tile) + 1


def build(nc, x, w_qkv, b_qkv, w_out, b_out, gate_w, gate_bias, Wg, Wu, Wd, Ws_g, Ws_u, Ws_d,
          c32, c16, out):
    with ExitStack() as ctx:
        def sb(name, shape, dt=F32):
            return ctx.enter_context(nc.sbuf_tensor(name, shape, dt))

        def sem(name):
            return ctx.enter_context(nc.semaphore(name))

        banks = [ctx.enter_context(nc.psum_tensor(f"bank{i}", [P, CH], F32)) for i in range(BANKS)]

        f32at, n32 = fields(C32)
        f16at, n16 = fields(C16)
        bfat, nbf = fields(CBF)
        k32, k16, kbf = sb("k32", [P, n32]), sb("k16", [P, n16], F16), sb("kbf", [P, nbf], BF16)

        def const32(name):
            return k32[:, f32at[name][0]:f32at[name][1]]

        def const16(name, g=0):
            return k16[:, f16at[name][0] + g * P:f16at[name][0] + (g + 1) * P]

        def constbf(name):
            return kbf[:, bfat[name][0]:bfat[name][1]]

        ident = const32("ident")
        vmask = const32("vmask").rearrange("p (g c) -> p g c", g=HG)
        stage = sb("stage", [P, 3, NUP, P])
        up_hi = sb("up_hi", [P, 2, NUP, P], F32R)
        up_lo = sb("up_lo", [P, 2, NUP, P], F32R)
        down_w = sb("down_w", [P, NUP, P])
        wqkv = sb("wqkv", [P, 3 * D])
        wqk_hi = sb("wqk_hi", [P, 2 * D], F32R)
        wqk_lo = sb("wqk_lo", [P, 2 * D], F32R)
        wout = sb("wout", [P, D])
        vectors = sb("vectors", [E + 4, D])
        turned = sb("turned", [P, E + 4])
        gateT, bk, bv, bo = turned[:, 0:E], turned[:, E + 1:E + 2], turned[:, E + 2:E + 3], turned[:, E + 3:E + 4]
        bq = sb("bq", [P, 1])
        bs = sb("bs", [P, 1])
        gb_row = sb("gb_row", [1, E])
        ones_row = sb("ones_row", [1, P])
        gb = sb("gb", [P, E])
        pairsel = sb("pairsel", [96, EP, P], F32R)
        repeat = sb("repeat", [P, 4, P], F32R)
        vn_hi = sb("vn_hi", [P, CH], F32R)
        vn_lo = sb("vn_lo", [P, CH], F32R)
        half = sb("half", [P, NT])
        xin = sb("xin", [P, NT, D])
        xres = sb("xres", [P, NT, D])
        st6 = sb("st6", [P, NT, 6])
        mv = sb("mv", [P, NT, 2])
        ve = sb("ve", [P, NT])
        y0 = sb("y0", [P, NT])
        nw = sb("nw", [P, NT])
        rstd = sb("rstd", [P, NT])
        xT = sb("xT", [P, S])
        xh = sb("xh", [P, S], F32R)
        xl = sb("xl", [P, S], F32R)
        qkh = sb("qkh", [P, 2, S], F16)
        qkl = sb("qkl", [P, 2, S], F16)
        vbd = sb("vbd", [P, NBLK, HG, 2 * BLK])
        qtmp = sb("qtmp", [P, S], F16)
        qpad = sb("qpad", [P, NBLK, 4, BLK], F16)
        qall = sb("qall", [P, 2, S], F16)
        kall = sb("kall", [P, 2, S], F16)
        kpad = sb("kpad", [P, 2, NBLK, 4, BLK], F16)
        mxp = sb("mxp", [P, 2, NBLK])
        maxd = sb("maxd", [P, NBLK, BLK], F16)
        prob = stage[:].rearrange("p k t m -> p (k t m)")[:, 0:NPROB * CH].rearrange("p (n q) -> p n q", n=NPROB)
        ctxT = sb("ctxT", [P, S])
        denT = sb("denT", [P, S])
        sT = sb("sT", [P, S])
        qkf = sT[:].rearrange("p (w q) -> p w q", w=2)
        z = sb("z", [P, S])
        th = sb("th", [P, NT, E])
        sc = sb("sc", [P, NT, E])
        sfc = sb("sfc", [P, NT, E])
        pm = sb("pm", [P, 4, NT, NGRP, 2])
        g2 = sb("g2", [P, 2, NT, NGRP])
        gs = sb("gs", [P, NT, NGRP])
        cmp_ = sb("cmp", [P, 2, NT, NGRP, NGRP])
        cnt = sb("cnt", [P, NT, NGRP])
        gm = sb("gm", [P, 2, NT, NGRP])
        msk = sb("msk", [P, NT, E])
        top = sb("top", [P, NT, 8])
        gt = sb("gt", [P, NT, E])
        eq = sb("eq", [P, NT, E])
        pre = sb("pre", [P, 2, NT, 2 * E])
        need = sb("need", [P, NT])
        cw = sb("cw", [P, NT, E])
        wsum = sb("wsum", [P, NT])
        cwT = sb("cwT", [96, S], F32R)
        k96 = ctxT[0:96]
        hid = sb("hid", [P, NHID, CH])
        wrow = sb("wrow", [P, NWT, CH])
        tz = sb("tz", [P, CH])

        filled = [sem(f"bank{i}_filled") for i in range(BANKS)]
        emptied = [sem(f"bank{i}_emptied") for i in range(BANKS)]
        k32_loaded = sem("k32_loaded")
        wqkv_loaded = sem("wqkv_loaded")
        k16_loaded = sem("k16_loaded")
        consts_ready = sem("consts_ready")
        hi_ready = sem("hi_ready")
        vn_hi_ready = sem("vn_hi_ready")
        cw_hi_ready = sem("cw_hi_ready")
        small_loaded = sem("small_loaded")
        weights_loaded = [sem(f"{name}_loaded") for name in ("gates", "ups", "downs")]
        fills_ready = sem("fills_ready")
        rec_ready = sem("rec_ready")
        small_ready = sem("small_ready")
        x_loaded = sem("x_loaded")
        xres_loaded = sem("xres_loaded")
        var_ready = sem("var_ready")
        pow_ready = sem("pow_ready")
        xn_ready = sem("xn_ready")
        xh_ready = sem("xh_ready")
        xl_ready = sem("xl_ready")
        lo_ready = sem("lo_ready")
        cw_ready = sem("cw_ready")
        qpad_ready = sem("qpad_ready")
        kpad_ready = sem("kpad_ready")
        max_ready = sem("max_ready")
        maxd_ready = sem("maxd_ready")
        pv_done = sem("pv_done")
        down_done = sem("down_done")
        tz_ready = sem("tz_ready")
        z2_ready = sem("z2_ready")
        ctx_ready = sem("ctx_ready")
        hid_ready = sem("hid_ready")
        tanh_ready = sem("tanh_ready")
        o_ready = sem("o_ready")
        stored = [sem(f"stored{c}") for c in range(NCH)]

        x_v = x.rearrange("b (t p) d -> b p t d", p=P)
        out_v = out.rearrange("b (t p) d -> b p t d", p=P)

        def chunk(c):
            return slice(CH * c, CH * (c + 1))

        def sections(eng, walk):
            walk(At(FIRST, 0))
            with eng.Fori(0, B - 1) as b:
                walk(At(BODY, b))
            walk(At(LAST, B - 1))

        def all_taken(eng, at, tiles, own=None):
            last = {at.bank(tile): tile for tile in tiles}
            for bank, tile in last.items():
                if bank != own:
                    eng.wait_ge(emptied[bank], at.taken(tile))

        block = ctx.enter_context(nc.Block())

        @block.sync
        def _(sp):
            sp.dma_start(xin[:], x_v[0]).then_inc(x_loaded, 16)
            sp.dma_start(wqkv[:], w_qkv).then_inc(wqkv_loaded, 16)
            for k, (w, ws) in enumerate(((Wg, Ws_g), (Wu, Ws_u))):
                sp.dma_start(stage[:, k, 0:EP, :], w.rearrange("(t e) i h -> (e i) t h", e=2)).then_inc(weights_loaded[k], 16)
                sp.dma_start(stage[:, k, EP, :], ws).then_inc(weights_loaded[k], 16)
            sp.dma_start(k16[:], c16).then_inc(k16_loaded, 16)
            sp.dma_start(stage[:, 2, 0:EP, :].rearrange("h t (e i) -> h (t e) i", e=2),
                         Wd.rearrange("e h i -> h e i")).then_inc(weights_loaded[2], 16)
            sp.dma_start(stage[:, 2, EP, :], Ws_d).then_inc(weights_loaded[2], 16)

            def of_batch(v, b):
                return v[b] if isinstance(b, int) else v[bass.ds(b, 1)].rearrange("a p t d -> p (a t) d")

            def batch(at):
                b = at.b
                if at.section is BODY:
                    sp.wait_ge(xl_ready, NCH * b + NCH)
                    sp.dma_start(xin[:], of_batch(x_v, b + 1)).then_inc(x_loaded, 16)
                for c in range(NCH):
                    sp.wait_ge(stored[c], 16 * b + 16)
                sp.dma_start(xres[:], of_batch(x_v, b)).then_inc(xres_loaded, 16)
                for c in range(NCH):
                    sp.wait_ge(emptied[at.bank(("outT", c))], at.taken(("outT", c)))
                    sp.dma_start(of_batch(out_v, b)[:, TPC * c:TPC * (c + 1), :], xres[:, TPC * c:TPC * (c + 1), :])\
                        .then_inc(stored[c], 16)

            with sp.Fori(0, B - 1) as b:
                batch(At(BODY, b))
            batch(At(LAST, B - 1))
            for c in range(NCH):
                sp.wait_ge(stored[c], 16 * (B + 1))

        @block.tensor
        def _(pe):
            def fill(at, tile):
                pe.wait_ge(emptied[at.bank(tile)], at.free(tile))
                return banks[at.bank(tile)]

            def done(at, tile, ins):
                ins.then_inc(filled[at.bank(tile)], 1)

            def parts3(ps, w_hi, w_lo, x_hi, x_lo):
                pe.matmul(ps[:], w_hi, x_hi, start=True, stop=False)
                pe.matmul(ps[:], w_lo, x_hi, start=False, stop=False)
                return pe.matmul(ps[:], w_hi, x_lo, start=False, stop=True)

            def walk(at):
                b, opened = at.b, set()
                for s in at.steps:
                    kind = s[0]
                    if kind == "weights":
                        if s[2] == 0:
                            pe.wait_ge(weights_loaded[s[1]], 2 * 16)
                        ps = fill(at, s)
                        for i in range(s[2], s[3]):
                            ins = pe.transpose(ps[:, P * (i - s[2]):P * (i - s[2] + 1)], stage[:, s[1], i, :], ident)
                        done(at, s, ins)
                    elif kind == "small":
                        pe.wait_ge(k32_loaded, 16)
                        pe.wait_ge(small_loaded, 5 * 16)
                        pe.wait_ge(small_ready, 1)
                        ps = fill(at, s)
                        pe.transpose(ps[:, 0:E + 4], vectors[:], ident[0:E + 4, 0:E + 4])
                        done(at, s, pe.matmul(ps[:, 32:32 + E], ones_row[:], gb_row[:], start=True, stop=True))
                    elif kind == "vbias":
                        all_taken(pe, at, [("small",)], at.bank(s))
                        ps = fill(at, s)
                        done(at, s, pe.matmul(ps[:, 0:1], wout[:], bv, start=True, stop=True))
                    elif kind == "xT":
                        c = s[1]
                        pe.wait_ge(xn_ready, at.next * NCH + (c + 1))
                        ps = fill(at, s)
                        for i in range(TPC):
                            ins = pe.transpose(ps[:, P * i:P * (i + 1)], xin[:, TPC * c + i, :], ident)
                        done(at, s, ins)
                    elif kind in ("q", "k"):
                        c, w = s[1], "qk".index(kind)
                        if kind == "q":
                            pe.wait_ge(xl_ready, at.next * NCH + (c + 1))
                            if at.section is FIRST and c == 0:
                                pe.wait_ge(small_ready, 2)
                        ps = fill(at, s)
                        done(at, s, parts3(ps, wqk_hi[:, D * w:D * (w + 1)], wqk_lo[:, D * w:D * (w + 1)],
                                           xh[:, chunk(c)], xl[:, chunk(c)]))
                    elif kind == "vn":
                        c = s[1]
                        pe.wait_ge(emptied[at.bank(("xT", c))], at.taken(("xT", c)))
                        ps = fill(at, s)
                        for i in range(TPC):
                            ins = pe.matmul(ps[:, D * i:D * (i + 1)], xT[:, CH * c + P * i:CH * c + P * (i + 1)],
                                            wqkv[:, 2 * D:3 * D], start=True, stop=True)
                        done(at, s, ins)
                    elif kind == "v":
                        c, i = s[1], s[2]
                        if i == 0:
                            pe.wait_ge(emptied[at.bank(("vn", c))], at.taken(("vn", c)))
                        ps = fill(at, s)
                        pe.matmul(ps[:], repeat[:, i, :], vn_hi[:], start=True, stop=False)
                        done(at, s, pe.matmul(ps[:], repeat[:, i, :], vn_lo[:], start=False, stop=True))
                    elif kind == "gate":
                        tiles = [("xT", i) for i in range(NCH)] + ([("small",)] if at.section is FIRST else [])
                        all_taken(pe, at, tiles, at.bank(s))
                        ps = fill(at, s)
                        for t in range(NT):
                            ins = pe.matmul(ps[:, E * t:E * (t + 1)], xT[:, P * t:P * (t + 1)], gateT,
                                            start=True, stop=True)
                        done(at, s, ins)
                    elif kind == "cwT":
                        c = s[1]
                        pe.wait_ge(cw_ready, at.next + 1)
                        ps = fill(at, s)
                        for i in range(TPC):
                            ins = pe.transpose(ps[0:E, P * i:P * (i + 1)], cw[:, TPC * c + i, :], ident)
                        done(at, s, ins)
                    elif kind in ("qsel", "ksel", "qfull"):
                        g, c = s[1], s[2]
                        of = b if g else at.next
                        w = 1 if kind == "ksel" else 0
                        if at.section is FIRST and c == 0 and kind == "qsel":
                            pe.wait_ge(k16_loaded, 16)
                        if g == 0 and c == 0 and kind == "qsel":
                            pe.wait_ge(lo_ready, of * 2 * NCH + 2 * NCH)
                        if kind == "qfull":
                            pe.wait_ge(maxd_ready, b * HG * NCH + (g * NCH + c + 1))
                        ps = fill(at, s)
                        if kind == "qfull":
                            pe.matmul(ps[:], const16("eye"), qtmp[:, chunk(c)], start=True, stop=False)
                            ins = pe.matmul(ps[:], const16("negmax"), maxd[:, BPC * c:BPC * (c + 1), :],
                                            start=False, stop=True)
                        else:
                            n = "qk"[w]
                            pe.matmul(ps[:], const16(n + "_a", g), qkh[:, w, chunk(c)], start=True, stop=False)
                            ins = pe.matmul(ps[:], const16(n + "_b", g), qkl[:, w, chunk(c)], start=False, stop=True)
                        done(at, s, ins)
                    elif kind == "max":
                        g, n = s[1], s[2]
                        of = b if g else at.next
                        if n == 0:
                            if at.section is FIRST:
                                pe.wait_ge(consts_ready, 1)
                            pe.wait_ge(qpad_ready, of * HG + (g + 1))
                            all_taken(pe, at, [("ksel", g, i) for i in range(NCH)], at.bank(s))
                        ps = fill(at, s)
                        if g == GLOBAL:
                            j, c, cols = GM[n]
                            last = CH * c + cols == BLK * (j + 1)
                            ins = pe.matmul(ps[:, 0:cols], qpad[:, j, :, :], kall[:, g % 2, CH * c:CH * c + cols],
                                            start=True, stop=not last, skip_group_check=True)
                            if last:
                                ins = pe.matmul(ps[:, cols - BLK:cols], constbf("identb"), constbf("win")[:, BLK:2 * BLK],
                                                start=False, stop=True, skip_group_check=True)
                        else:
                            pe.matmul(ps[:], constbf("identb"), constbf("win0" if n == 0 else "win"), start=True, stop=False,
                                      skip_group_check=True)
                            for i in range(LOC):
                                j = LOC * n + i
                                lo = max(0, BLK * (j - 1))
                                cols = BLK * (j + 1) - lo
                                ins = pe.matmul(ps[:, 2 * BLK * (i + 1) - cols:2 * BLK * (i + 1)], qpad[:, j, :, :],
                                                kall[:, g % 2, lo:lo + cols], start=False, stop=(i == LOC - 1),
                                                skip_group_check=True)
                        done(at, s, ins)
                    elif kind == "score":
                        g, n = s[1], s[2]
                        if n == 0 and g != GLOBAL:
                            all_taken(pe, at, [("qfull", g, i) for i in range(NCH)], at.bank(s))
                        elif g == GLOBAL and n in (0, CUT):
                            all_taken(pe, at, [("qfull", g, int(n == CUT))], at.bank(s))
                        if n == 0:
                            pe.wait_ge(kpad_ready, b * HG + (g + 1))
                        ps = fill(at, s)
                        if g == GLOBAL:
                            j, c, q0, cols = GT[n]
                            diag = q0 == BLK * j
                            ins = pe.matmul(ps[:, 0:cols], kpad[:, g % 2, j, :, :], qall[:, g % 2, q0:q0 + cols],
                                            start=True, stop=not diag, skip_group_check=True)
                            if diag:
                                ins = pe.matmul(ps[:, 0:BLK], constbf("identb"), constbf("win")[:, 0:BLK],
                                                start=False, stop=True, skip_group_check=True)
                        else:
                            pe.matmul(ps[:], constbf("identb"), constbf("win"), start=True, stop=False,
                                      skip_group_check=True)
                            for i in range(LOC):
                                j = LOC * n + i
                                cols = min(2 * BLK, S - BLK * j)
                                ins = pe.matmul(ps[:, 2 * BLK * i:2 * BLK * i + cols], kpad[:, g % 2, j, :, :],
                                                qall[:, g % 2, BLK * j:BLK * j + cols], start=False, stop=(i == LOC - 1),
                                                skip_group_check=True)
                        done(at, s, ins)
                    elif kind == "pv":
                        g, n = s[1], s[2]
                        t = SCORES_BEFORE[g] + n
                        half = int(g == GLOBAL and n >= CUT)
                        sums = ("acc", g, half)
                        if n == CUT * half:
                            fill(at, sums)
                            opened = set()
                        acc = banks[at.bank(sums)]
                        tile = ("score", g, n)
                        pe.wait_ge(emptied[at.bank(tile)], at.taken(tile))
                        pieces = []
                        if g == GLOBAL:
                            j, c, q0, cols = GT[n]
                            spans = [(j, q0, 0, cols)]
                        else:
                            spans = [(j, BLK * j, 2 * BLK * (j - LOC * n), min(2 * BLK, S - BLK * j))
                                     for j in range(LOC * n, LOC * (n + 1))]
                        for j, q0, col, cols in spans:
                            q = q0
                            while q < q0 + cols:
                                to = min(q0 + cols, (q // QTR + 1) * QTR)
                                pieces.append((j, q // QTR, q, col + q - q0, to - q))
                                q = to
                        for j, qt, q, col, cols in pieces:
                            r, o = 64 * (qt % 2), QTR * (qt // 2 - half) + q % QTR
                            ins = pe.matmul(acc[r:r + 64, o:o + cols], vbd[:, j, HEADS[g], :], prob[:, t % NPROB, col:col + cols],
                                            start=r not in opened, stop=False, skip_group_check=True)
                            opened.add(r)
                        ins.then_inc(pv_done, 1)
                    elif kind == "proj":
                        c = s[1]
                        pe.wait_ge(ctx_ready, b * 2 * NCH + (2 * c + 2))
                        ps = fill(at, s)
                        done(at, s, pe.matmul(ps[:], wout[:], ctxT[:, chunk(c)], start=True, stop=True))
                    elif kind == "up":
                        c, t = s[1], s[2]
                        x_hi, x_lo = xh[:, chunk(c)], xl[:, chunk(c)]
                        first = c == 0 and t == 0
                        for x in ("gate", "up", "weight") if first else ("weight", "gate", "up"):
                            if x == "weight" and t < EP:
                                if first:
                                    all_taken(pe, at, [("cwT", i) for i in range(NCH)])
                                ps = fill(at, s + (x,))
                                done(at, s + (x,), pe.matmul(ps[:], pairsel[:, t, :], cwT[:, chunk(c)], start=True, stop=True))
                            elif x != "weight":
                                k = ("gate", "up").index(x)
                                ps = fill(at, s + (x,))
                                done(at, s + (x,), parts3(ps, up_hi[:, k, t, :], up_lo[:, k, t, :], x_hi, x_lo))
                    elif kind == "down":
                        c, t = s[1], s[2]
                        of = at.of(s)
                        i = NUP * c + t
                        if t == 0:
                            fill(at, ("y", c))
                        if t < EP:
                            pe.wait_ge(hid_ready, of * NCH * EP + (EP * c + t + 1))
                        else:
                            up = ("up", c, t, "up")
                            pe.wait_ge(emptied[at.bank(up)], at.taken(up))
                        pe.matmul(banks[Y][:], down_w[:, t, :], hid[:, i % NHID, :],
                                  start=(t == 0), stop=(t == NUP - 1)).then_inc(down_done, 1)
                    elif kind == "outT":
                        c = s[1]
                        pe.wait_ge(o_ready, b * NCH + (c + 1))
                        ps = fill(at, s)
                        for i in range(TPC):
                            ins = pe.transpose(ps[:, P * i:P * (i + 1)], sT[:, CH * c + P * i:CH * c + P * (i + 1)], ident)
                        done(at, s, ins)

            sections(pe, walk)

        @block.scalar
        def _(act):
            act.dma_start(k32[:], c32).then_inc(k32_loaded, 16)
            act.dma_start(vectors[0:E, :], gate_w).then_inc(small_loaded, 16)
            act.dma_start(vectors[E:E + 3, :], b_qkv.rearrange("(k p) -> k p", k=3)).then_inc(small_loaded, 16)
            act.dma_start(vectors[E + 3:E + 4, :], b_out.rearrange("(a p) -> a p", a=1)).then_inc(small_loaded, 16)
            act.dma_start(gb_row[:], gate_bias.rearrange("(a e) -> a e", a=1)).then_inc(small_loaded, 16)
            act.dma_start(wout[:], w_out).then_inc(small_loaded, 16)

            def walk(at):
                b = at.b
                for s in at.steps:
                    kind = s[0]
                    if kind == "setup":
                        act.wait_ge(k32_loaded, 16)
                        act.activation(constbf("identb"), ident, ACT.Copy)
                        for name, first in (("win", "win"), ("win0", "win0")):
                            tile = constbf(name).rearrange("p (j q) -> p j q", q=2 * BLK)
                            act.activation(tile[:, 1:LOC], const32("win").unsqueeze(1).broadcast_to([P, LOC - 1, 2 * BLK]), ACT.Copy)
                            act.activation(tile[:, 0], const32(first), ACT.Copy)
                        act.activation(repeat[:].rearrange("p i (a q) -> p i a q", a=4),
                                       ident.rearrange("p (i q) -> p i q", i=4).unsqueeze(2).broadcast_to([P, 4, 4, BLK]), ACT.Copy)
                        act.activation(pairsel[:].rearrange("p t (e i) -> p (t e) i", e=2),
                                       const32("eye32")[0:96, 0:E].unsqueeze(2).broadcast_to([96, E, I]), ACT.Copy, scale=0.5)\
                            .then_inc(consts_ready, 1)
                        continue
                    if kind == "ones":
                        act.wait_ge(k32_loaded, 16)
                        act.activation(vbd[:, :, :, BLK:2 * BLK].rearrange("p j g c -> p j (g) c"),
                                       vmask.unsqueeze(1).broadcast_to([P, NBLK, HG, BLK]), ACT.Copy).then_inc(consts_ready, 1)
                        continue
                    if kind == "weights":
                        k, lo, hi = s[1], s[2], s[3]
                        tile = banks[at.bank(s)][:, 0:P * (hi - lo)].rearrange("p (t m) -> p t m", m=P)
                        act.wait_ge(filled[at.bank(s)], at.filled(s))
                        if k < 2:
                            act.activation(up_hi[:, k, lo:hi, :], tile, ACT.Copy).then_inc(hi_ready, 1)
                        else:
                            act.activation(down_w[:, lo:hi, :], tile, ACT.Copy, scale=0.5 if hi == NUP else 1.0)\
                                .then_inc(emptied[at.bank(s)], 1)
                        continue
                    if kind == "up":
                        c, t = s[1], s[2]
                        i = NUP * c + t
                        of = at.of(s)
                        gate, weight = s + ("gate",), s + ("weight",)
                        act.wait_ge(filled[at.bank(gate)], at.filled(gate))
                        if i >= NHID:
                            act.wait_ge(down_done, of * NCH * NUP + (i - NHID + 1))
                        act.activation(hid[:, i % NHID, :], banks[at.bank(gate)][:], ACT.Tanh, scale=0.5).then_inc(tanh_ready, 1)
                        if t < EP:
                            iw = EP * c + t
                            act.wait_ge(filled[at.bank(weight)], at.filled(weight))
                            if iw >= NWT:
                                act.wait_ge(hid_ready, of * NCH * EP + (iw - NWT + 1))
                            act.activation(wrow[:, iw % NWT, :], banks[at.bank(weight)][:], ACT.Copy)\
                                .then_inc(emptied[at.bank(weight)], 1)
                        continue
                    if kind == "z":
                        c = s[1]
                        act.wait_ge(emptied[Y], at.taken(("z", c)))
                        act.activation(tz[:], z[:, chunk(c)], ACT.Tanh, scale=0.5).then_inc(tz_ready, 1)
                        continue
                    if kind == "norm":
                        g, c = s[1], s[2]
                        done = SCORES_BEFORE[g] + CUT if g == GLOBAL and c == 0 else SCORES_BEFORE[g + 1]
                        act.wait_ge(pv_done, b * SCORES_BEFORE[HG] + done)
                        acc, heads = banks[at.bank(("acc", g, c))], slice(32 * HEADS[g], 32 * HEADS[g] + 32)
                        for u in range(2):
                            for part, to in enumerate((ctxT, denT)):
                                r = 64 * u + 32 * part
                                if g == GLOBAL:
                                    q = CH * c + QTR * u
                                    ins = act.activation(to[heads, q:q + QTR], acc[r:r + 32, 0:QTR], ACT.Copy)
                                else:
                                    ins = act.activation(to[heads, :].rearrange("p (v u q) -> p u v q", u=2, q=QTR)[:, u],
                                                         acc[r:r + 32, :].rearrange("p (v q) -> p v q", q=QTR), ACT.Copy)
                        ins.then_inc(emptied[at.bank(("acc", g, c))], 1)
                        continue
                    if kind in ("vn", "cwT"):
                        act.wait_ge(filled[at.bank(s)], at.filled(s))
                        if kind == "vn":
                            act.activation(vn_hi[:], banks[at.bank(s)][:], ACT.Copy).then_inc(vn_hi_ready, 1)
                        else:
                            act.activation(cwT[0:E, chunk(s[1])], banks[at.bank(s)][0:E, :], ACT.Copy).then_inc(cw_hi_ready, 1)
                        continue
                    if kind not in ("xT", "q", "k", "gate", "qsel", "ksel", "qfull", "score", "proj"):
                        continue
                    ps, freed = banks[at.bank(s)], emptied[at.bank(s)]
                    act.wait_ge(filled[at.bank(s)], at.filled(s))
                    if kind == "q" and at.section is FIRST and s[1] == 0:
                        act.wait_ge(emptied[at.bank(("small",))], at.taken(("small",)))
                    if kind == "xT":
                        act.activation(xT[:, chunk(s[1])], ps[:], ACT.Copy).then_inc(freed, 1)
                    elif kind in ("q", "k"):
                        w, c = "qk".index(kind), s[1]
                        scale, bias = (Q_SCALE, bq[:]) if kind == "q" else (1.0, bk)
                        if c:
                            act.wait_ge(lo_ready, at.next * 2 * NCH + (2 * c + w - 1))
                        act.activation(qkf[:, w, :], ps[:], ACT.Identity, bias=bias, scale=scale)
                        act.activation(qkh[:, w, chunk(c)], ps[:], ACT.Identity, bias=bias, scale=scale).then_inc(freed, 1)
                    elif kind == "gate":
                        act.activation(th[:].rearrange("p t e -> p (t e)"), ps[:, 0:NT * E], ACT.Tanh, scale=0.5)\
                            .then_inc(freed, 1)
                    elif kind == "qsel":
                        act.activation(qtmp[:, chunk(s[2])], ps[:], ACT.Copy).then_inc(freed, 1)
                    elif kind == "ksel":
                        act.activation(kall[:, s[1] % 2, chunk(s[2])], ps[:], ACT.Identity, bias=const32("onerow"))\
                            .then_inc(freed, 1)
                    elif kind == "qfull":
                        act.activation(qall[:, s[1] % 2, chunk(s[2])], ps[:], ACT.Copy).then_inc(freed, 1)
                    elif kind == "score":
                        g, n = s[1], s[2]
                        t = SCORES_BEFORE[g] + n
                        cols = GT[n][3] if g == GLOBAL else CH
                        if t >= NPROB:
                            act.wait_ge(pv_done, b * SCORES_BEFORE[HG] + (t - NPROB + 1))
                        act.activation(prob[:, t % NPROB, 0:cols], ps[:, 0:cols], ACT.Exp).then_inc(freed, 1)
                    elif kind == "proj":
                        act.activation(sT[:, chunk(s[1])], ps[:], ACT.Identity, bias=bs[:], scale=0.5).then_inc(freed, 1)

            sections(act, walk)

        @block.vector
        def _(dve):
            def credits():
                for r in emptied:
                    dve.sem_inc(r, 1)
                for st in stored:
                    dve.sem_inc(st, 16)
                dve.memset(ones_row[:], 1.0).then_inc(small_ready, 1)
                dve.memset(qpad[:], 0.0)

            def setup():
                dve.wait_ge(wqkv_loaded, 16)
                dve.tensor_copy(wqk_hi[:], wqkv[:, 0:2 * D])
                dve.drain()
                dve.tensor_tensor(wqk_lo[:], wqkv[:, 0:2 * D], wqk_hi[:].bitcast(F32), ALU.subtract)\
                    .then_inc(small_ready, 1)

            def tt(out_, a, b_, op):
                return dve.tensor_tensor(out_, a, b_, op)

            def ts(out_, a, s1, s2, op0, op1=None):
                return dve.tensor_scalar(out_, a, s1, s2, op0, op1) if op1 else dve.tensor_scalar(out_, a, s1, s2, op0)

            def routing(part):
                def over(a, shape, axis):
                    return a.unsqueeze(axis).broadcast_to(shape)

                NG = [P, NT, NGRP, NGRP]
                pairs = sfc[:].rearrange("p t (g a b) -> p (t g) a b", g=NGRP, a=2)
                flat = [pm[:, i].rearrange("p t g a -> p (t g) a") for i in range(4)]
                g2f = [g2[:, i].rearrange("p t g -> p (t g)") for i in range(2)]
                other, own = over(gs[:], NG, 2), over(gs[:], NG, 3)
                lower = const32("lower").rearrange("p (i j) -> p i j", i=NGRP)
                of_group = "p t (g e) -> p t g e"
                kth = top[:, :, TOPK - 1:TOPK].broadcast_to([P, NT, E])
                run = pre[:, 0, :, E:2 * E]
                if part == 0:
                    ts(sc[:], th[:], 0.5, 0.5, ALU.mult, ALU.add)
                    dve.drain()
                    tt(sfc[:], sc[:], over(gb[:], [P, NT, E], 1), ALU.add)
                    dve.drain()
                    tt(flat[0], pairs[:, :, :, 0], pairs[:, :, :, 1], ALU.max)
                    tt(flat[1], pairs[:, :, :, 0], pairs[:, :, :, 1], ALU.min)
                    dve.drain()
                    tt(g2f[0], flat[0][:, :, 0], flat[0][:, :, 1], ALU.max)
                    tt(flat[2][:, :, 0], flat[0][:, :, 0], flat[0][:, :, 1], ALU.min)
                    tt(flat[2][:, :, 1], flat[1][:, :, 0], flat[1][:, :, 1], ALU.max)
                elif part == 1:
                    dve.drain()
                    tt(g2f[1], flat[2][:, :, 0], flat[2][:, :, 1], ALU.max)
                    dve.drain()
                    tt(gs[:], g2[:, 0], g2[:, 1], ALU.add)
                    dve.drain()
                    tt(cmp_[:, 0], other, own, ALU.is_gt)
                    tt(cmp_[:, 1], other, own, ALU.is_ge)
                    dve.drain()
                    tt(cmp_[:, 1], cmp_[:, 1], cmp_[:, 0], ALU.subtract)
                elif part == 2:
                    dve.drain()
                    tt(cmp_[:, 1], cmp_[:, 1], over(lower, NG, 1), ALU.mult)
                    dve.drain()
                    tt(cmp_[:, 0], cmp_[:, 0], cmp_[:, 1], ALU.add)
                    dve.drain()
                    dve.tensor_reduce(cnt[:], cmp_[:, 0], AX_X, ALU.add)
                    dve.drain()
                    ts(gm[:, 0], cnt[:], float(TOPG), None, ALU.is_lt)
                    ts(gm[:, 1], cnt[:], float(TOPG), -1e30, ALU.is_ge, ALU.mult)
                elif part == 3:
                    dve.drain()
                    tt(msk[:].rearrange(of_group, g=NGRP), sfc[:].rearrange(of_group, g=NGRP), over(gm[:, 0], NG, 3), ALU.mult)
                    dve.drain()
                    tt(msk[:].rearrange(of_group, g=NGRP), msk[:].rearrange(of_group, g=NGRP), over(gm[:, 1], NG, 3), ALU.add)
                    dve.drain()
                    for t in range(NT):
                        dve.max(top[:, t, :], msk[:, t, :])
                    dve.drain()
                    tt(gt[:], msk[:], kth, ALU.is_gt)
                    tt(eq[:], msk[:], kth, ALU.is_equal)
                    tt(pre[:, 0, :, E:2 * E], msk[:], kth, ALU.is_equal)
                elif part == 4:
                    dve.drain()
                    dve.tensor_reduce(need[:], gt[:], AX_X, ALU.add)
                    src = 0
                    for sh in (1, 2, 4, 8):
                        tt(pre[:, 1 - src, :, E:2 * E], pre[:, src, :, E:2 * E], pre[:, src, :, E - sh:2 * E - sh], ALU.add)
                        dve.drain()
                        src = 1 - src
                    tt(run, run, over(need[:], [P, NT, E], 2), ALU.add)
                    dve.drain()
                    ts(run, run, float(TOPK), None, ALU.is_le)
                    dve.drain()
                    tt(eq[:], eq[:], run, ALU.mult)
                elif part == 5:
                    dve.drain()
                    tt(gt[:], gt[:], eq[:], ALU.add)
                    dve.drain()
                    tt(msk[:], sc[:], gt[:], ALU.mult)
                    dve.drain()
                    dve.tensor_reduce(need[:], msk[:], AX_X, ALU.add)
                    dve.drain()
                    ts(need[:], need[:], 1e-20, None, ALU.add)
                elif part == 6:
                    dve.drain()
                    dve.reciprocal(wsum[:], need[:])
                    dve.drain()
                    dve.scalar_tensor_tensor(out=cw[:], in0=msk[:], scalar=ROUTE_SCALE, in1=over(wsum[:], [P, NT, E], 2),
                                             op0=ALU.mult, op1=ALU.mult).then_inc(cw_ready, 1)


            def walk(at):
                b = at.b
                if at.section is FIRST:
                    credits()
                for s in at.steps:
                    kind = s[0]
                    if kind == "stats":
                        dve.wait_ge(x_loaded, at.next * 16 + 16)
                        for t in range(NT):
                            dve.bn_stats(st6[:, t, :], xin[:, t, :])
                        dve.drain()
                        for t in range(NT):
                            dve.bn_aggr(mv[:, t, :], st6[:, t, :])
                        dve.drain()
                        ts(ve[:], mv[:, :, 1], LN_EPS, None, ALU.add).then_inc(var_ready, 1)
                    elif kind == "ln":
                        c = s[1]
                        if c == 0:
                            dve.wait_ge(pow_ready, at.next + 1)
                            tt(nw[:], y0[:], y0[:], ALU.mult)
                            dve.drain()
                            tt(nw[:], nw[:], ve[:], ALU.mult)
                            dve.drain()
                            ts(nw[:], nw[:], -0.5, 1.5, ALU.mult, ALU.add)
                            dve.drain()
                            tt(rstd[:], y0[:], nw[:], ALU.mult)
                            dve.drain()
                        for t in range(TPC * c, TPC * (c + 1)):
                            ins = ts(xin[:, t, :], xin[:, t, :], mv[:, t, 0:1], rstd[:, t:t + 1], ALU.subtract, ALU.mult)
                        ins.then_inc(xn_ready, 1)
                    elif kind == "xT":
                        dve.wait_ge(emptied[at.bank(s)], at.taken(s))
                        dve.tensor_copy(xh[:, chunk(s[1])], xT[:, chunk(s[1])]).then_inc(xh_ready, 1)
                    elif kind == "pads":
                        g = s[1]
                        all_taken(dve, at, [("qsel", g, i) for i in range(NCH)])
                        for h in range(4):
                            r = slice(32 * h, 32 * h + 32)
                            ins = dve.tensor_copy(qpad[r, :, h, :], qtmp[r, :].rearrange("p (j q) -> p j q", q=BLK))
                        ins.then_inc(qpad_ready, 1)
                    elif kind in ("maxdone", "kpads"):
                        g = s[1]
                        if kind == "maxdone":
                            if g != GLOBAL or s[2] == 0:
                                continue
                            dve.drain()
                            tt(mxp[:, 0, BPC:NBLK], mxp[:, 0, BPC:NBLK], mxp[:, 1, BPC:NBLK], ALU.max).then_inc(max_ready, 1)
                            continue
                        all_taken(dve, at, [("ksel", g, i) for i in range(NCH)])
                        for h in range(4):
                            r = slice(32 * h, 32 * h + 32)
                            ins = dve.tensor_copy(kpad[r, g % 2, :, h, :], kall[r, g % 2, :].rearrange("p (j q) -> p j q", q=BLK))
                        ins.then_inc(kpad_ready, 1)
                    elif kind == "fill":
                        dve.memset(kpad[:, s[1]], 0.0)
                        if s[1] == 1:
                            dve.wait_ge(fills_ready, 1)
                            dve.tensor_copy(cwT[:], k96)
                    elif kind == "setup":
                        setup()
                    elif kind == "route":
                        if s[1] == 0:
                            dve.wait_ge(emptied[at.bank(("gate",))], at.taken(("gate",)))
                        routing(s[1])
                    elif kind == "ctx":
                        c, q = s[1], CH * s[1] + QTR * s[2]
                        sums = ("acc", GLOBAL, c)
                        dve.wait_ge(emptied[at.bank(sums)], at.taken(sums))
                        dve.reciprocal(denT[:, q:q + QTR], denT[:, q:q + QTR]).then_inc(rec_ready, 1)
                    elif kind == "z":
                        c = s[1]
                        of = at.of(s)
                        dve.wait_ge(down_done, of * NCH * NUP + NUP * (c + 1))
                        tt(z[:, chunk(c)], xT[:, chunk(c)], banks[Y][:], ALU.add).then_inc(emptied[Y], 1)
                    elif kind == "z2":
                        c = s[1]
                        dve.wait_ge(tz_ready, at.of(s) * NCH + (c + 1))
                        dve.scalar_tensor_tensor(out=z[:, chunk(c)], in0=tz[:], scalar=1.0, in1=z[:, chunk(c)],
                                                 op0=ALU.add, op1=ALU.mult).then_inc(z2_ready, 1)
                    elif kind == "up":
                        i = NUP * s[1] + s[2]
                        gate = s + ("gate",)
                        dve.wait_ge(tanh_ready, at.of(s) * NCH * NUP + (i + 1))
                        dve.scalar_tensor_tensor(out=hid[:, i % NHID, :], in0=hid[:, i % NHID, :], scalar=1.0,
                                                 in1=banks[at.bank(gate)][:], op0=ALU.add, op1=ALU.mult)\
                            .then_inc(emptied[at.bank(gate)], 1)
                    elif kind == "times":
                        c, t = s[1], s[2]
                        i = NUP * c + t
                        gate, up = ("up", c, t, "gate"), ("up", c, t, "up")
                        dve.wait_ge(emptied[at.bank(gate)], at.taken(gate))
                        dve.wait_ge(filled[at.bank(up)], at.filled(up))
                        tt(hid[:, i % NHID, :], hid[:, i % NHID, :], banks[at.bank(up)][:], ALU.mult)\
                            .then_inc(emptied[at.bank(up)], 1)
                    elif kind == "weights" and s[1] == 2:
                        continue
                    elif kind in ("weights", "small", "vbias", "vn", "v", "cwT", "max", "outT"):
                        ps, freed = banks[at.bank(s)], emptied[at.bank(s)]
                        dve.wait_ge(filled[at.bank(s)], at.filled(s))
                        if kind == "weights":
                            k, lo, hi = s[1], s[2], s[3]
                            tile = ps[:, 0:P * (hi - lo)].rearrange("p (t m) -> p t m", m=P)
                            dve.wait_ge(hi_ready, WEIGHT_TILES.index(s) + 1)
                            tt(up_lo[:, k, lo:hi, :], tile, up_hi[:, k, lo:hi, :].bitcast(F32), ALU.subtract).then_inc(freed, 1)
                        elif kind == "small":
                            dve.tensor_copy(turned[:], ps[:, 0:E + 4])
                            ts(bq[:], ps[:, E:E + 1], Q_SCALE, None, ALU.mult)
                            dve.tensor_copy(gb[:], ps[:, 32:32 + E]).then_inc(freed, 1)
                        elif kind == "vbias":
                            ts(bs[:], ps[:, 0:1], bo, 0.5, ALU.add, ALU.mult).then_inc(freed, 1)
                        elif kind == "vn":
                            dve.wait_ge(vn_hi_ready, at.next * NCH + s[1] + 1)
                            tt(vn_lo[:], ps[:], vn_hi[:].bitcast(F32), ALU.subtract).then_inc(freed, 1)
                        elif kind == "v":
                            c, i = s[1], s[2]
                            tt(vbd[:].rearrange("p (t i) g c -> p i t g c", i=4)[:, i, TPC * c:TPC * (c + 1), :, 0:BLK],
                               ps[:].rearrange("p (j g c) -> p j g c", j=4, g=HG),
                               vmask.unsqueeze(1).broadcast_to([P, 4, HG, BLK]), ALU.mult).then_inc(freed, 1)
                        elif kind == "cwT":
                            c = s[1]
                            dve.wait_ge(cw_hi_ready, at.next * NCH + c + 1)
                            tt(cwT[32:32 + E, chunk(c)], ps[0:E, :], cwT[0:E, chunk(c)].bitcast(F32), ALU.subtract).then_inc(freed, 1)
                        elif kind == "max":
                            g, n = s[1], s[2]
                            if g == GLOBAL:
                                j, c, cols = GM[n]
                                ins = dve.tensor_reduce(mxp[:, c, j:j + 1], ps[:, 0:cols], AX_X, ALU.max)
                            else:
                                ins = dve.tensor_reduce(mxp[:, 0, LOC * n:LOC * (n + 1)],
                                                        ps[:].rearrange("p (j q) -> p j q", q=2 * BLK), AX_X, ALU.max)
                            ins.then_inc(freed, 1)
                        elif kind == "outT":
                            c = s[1]
                            dve.wait_ge(xres_loaded, b * 16 + 16)
                            tt(xres[:, TPC * c:TPC * (c + 1), :], xres[:, TPC * c:TPC * (c + 1), :],
                               ps[:].rearrange("p (t d) -> p t d", d=D), ALU.add).then_inc(freed, 1)

            sections(dve, walk)

        @block.gpsimd
        def _(pool):
            def walk(at):
                b = at.b
                if at.section is FIRST:
                    pool.memset(half[:], -0.5)
                    pool.memset(pre[:], 0.0)
                    pool.memset(k96, 0.0).then_inc(fills_ready, 1)
                    pool.drain()
                for s in at.steps:
                    kind = s[0]
                    if kind == "stats":
                        pool.wait_ge(var_ready, at.next + 1)
                        pool.tensor_tensor(y0[:], ve[:], half[:], ALU.pow).then_inc(pow_ready, 1)
                    elif kind == "xT":
                        c = s[1]
                        pool.wait_ge(xh_ready, at.next * NCH + (c + 1))
                        pool.tensor_tensor(xl[:, chunk(c)], xT[:, chunk(c)], xh[:, chunk(c)].bitcast(F32), ALU.subtract)\
                            .then_inc(xl_ready, 1)
                    elif kind in ("q", "k"):
                        w, c = "qk".index(kind), s[1]
                        pool.wait_ge(emptied[at.bank(s)], at.taken(s))
                        pool.tensor_tensor(qkl[:, w, chunk(c)], qkf[:, w, :], qkh[:, w, chunk(c)], ALU.subtract)\
                            .then_inc(lo_ready, 1)
                    elif kind == "maxdone":
                        g, c = s[1], s[2]
                        if g == GLOBAL and c == 1:
                            pool.wait_ge(max_ready, b + 1)
                        else:
                            tile = ("max", g, CUT - 1 if g == GLOBAL else MAXES[g] // 2 * (c + 1) - 1)
                            pool.wait_ge(emptied[at.bank(tile)], at.taken(tile))
                        blocks = slice(BPC * c, BPC * (c + 1))
                        pool.tensor_tensor(maxd[:, blocks, :], mxp[:, 0, blocks].unsqueeze(2).broadcast_to([P, BPC, BLK]),
                                           const32("eye32").unsqueeze(1).broadcast_to([P, BPC, BLK]), ALU.mult)\
                            .then_inc(maxd_ready, 1)
                    elif kind == "times" and s[2] < EP:
                        c, t = s[1], s[2]
                        up, weight = ("up", c, t, "up"), ("up", c, t, "weight")
                        i, iw = NUP * c + t, EP * c + t
                        pool.wait_ge(emptied[at.bank(weight)], at.taken(weight))
                        pool.wait_ge(emptied[at.bank(up)], at.taken(up))
                        pool.tensor_tensor(hid[:, i % NHID, :], hid[:, i % NHID, :], wrow[:, iw % NWT, :], ALU.mult)\
                            .then_inc(hid_ready, 1)
                    elif kind == "ctx":
                        q = CH * s[1] + QTR * s[2]
                        pool.wait_ge(rec_ready, b * 2 * NCH + (2 * s[1] + s[2] + 1))
                        pool.tensor_tensor(ctxT[:, q:q + QTR], ctxT[:, q:q + QTR], denT[:, q:q + QTR], ALU.mult)\
                            .then_inc(ctx_ready, 1)
                    elif kind == "mul":
                        c = s[1]
                        pool.wait_ge(z2_ready, b * NCH + (c + 1))
                        pool.wait_ge(emptied[at.bank(("proj", c))], at.taken(("proj", c)))
                        pool.tensor_tensor(sT[:, chunk(c)], sT[:, chunk(c)], z[:, chunk(c)], ALU.mult).then_inc(o_ready, 1)

            sections(pool, walk)


_INS = ["L0_attn_x", "L0_attn_w_qkv", "L0_attn_b_qkv", "L0_attn_w_out", "L0_attn_b_out", "L0_ffn_gate_w",
        "L0_ffn_gate_bias", "L0_ffn_Wg", "L0_ffn_Wu", "L0_ffn_Wd", "L0_ffn_Ws_g", "L0_ffn_Ws_u", "L0_ffn_Ws_d"]
_OUTS = [((B, S, D), "float32")]


def constants():
    import numpy as np

    rows, cols = np.arange(P)[:, None], np.arange(P)[None, :]
    head, r = rows // BLK, rows % BLK
    f32 = {
        "ident": rows == cols,
        "vmask": np.tile(head == np.arange(BLK)[None, :] // HD, (1, HG)),
        "eye32": r == np.arange(BLK)[None, :],
        "onerow": r == 3 * HD,
    }
    f32 |= {
        "lower": np.tile((np.arange(NGRP)[None, :] < np.arange(NGRP)[:, None]).reshape(1, -1), (P, 1)),
    }
    feature_head, dim = rows // HD, rows % HD

    def select(g, groups):
        out = np.zeros((P, P), bool)
        for part in groups:
            out |= cols == (feature_head - 4 * g) * BLK + part * HD + dim
        return out & (feature_head // 4 == g)

    f16 = {name: np.concatenate([select(g, groups) for g in HEADS], 1)
           for name, groups in (("q_a", (0, 2)), ("q_b", (1,)), ("k_a", (0, 1)), ("k_b", (2,)))}
    f16["eye"] = rows == cols
    f16["negmax"] = -1.0 * (cols == head * BLK + 3 * HD)
    c = np.arange(2 * BLK)[None, :]
    inside = (c >= r) & (c <= r + WINDOW)
    f32 |= {"win": np.where(inside, 0.0, -1e30), "win0": np.where(inside & (c >= BLK), 0.0, -1e30)}

    def packed(parts, sizes, dtype):
        return np.concatenate([np.asarray(parts[n]).astype(dtype) for n in sizes], 1)

    return {"c32": packed(f32, C32, np.float32),
            "c16": packed(f16, C16, np.float16)}


def kernel(**inputs):
    import numpy as _np
    import concourse.bacc as _bacc
    from concourse import mybir as _mybir
    from concourse.bass_utils import run_bass_kernel_spmd as _run

    nc = _bacc.Bacc("TRN2", target_bir_lowering=False, num_devices=1)
    arrays, args = {}, []
    for name, a in [(n, _np.ascontiguousarray(inputs[n])) for n in _INS] + list(constants().items()):
        arrays[f"in_{name}_dram"] = a
        args.append(nc.dram_tensor(f"in_{name}_dram", a.shape, _mybir.dt.from_np(a.dtype), kind="ExternalInput").ap())
    for i, (shape, dtype) in enumerate(_OUTS):
        dt = _mybir.dt.from_np(_np.dtype(dtype))
        args.append(nc.dram_tensor(f"out_{i}_dram", shape, dt, kind="ExternalOutput").ap())
    build(nc, *args)
    r = _run(nc, [arrays], core_ids=[0])
    got = tuple(r.results[0][f"out_{i}_dram"] for i in range(len(_OUTS)))
    return got[0]
```
